# Optimizing a Trainium2 kernel written in Bass

```python
import numpy as np
import jax
import jax.numpy as jnp

def _softmax(x, axis=-1):
    return jax.nn.softmax(x, axis=axis)

def _gelu(x):
    return jax.nn.gelu(x, approximate=True)

def _silu(x):
    return jax.nn.silu(x)

def _sigmoid(x):
    return jax.nn.sigmoid(x)

def _layernorm(x, axis=-1, eps=1e-05):
    m = jnp.mean(x, axis=axis, keepdims=True)
    v = jnp.var(x, axis=axis, keepdims=True)
    return (x - m) / jnp.sqrt(v + eps)

def _scatter_add(tgt, idx, src, axis=0):
    return tgt.at[idx].add(src)

def _segment_sum(src, seg, n):
    return jax.ops.segment_sum(src, seg, n)
kernel_name = 'mk_prb_d1_jaxref_r4_5f0852'

def setup_inputs(seed: int=0):
    np.random.seed(seed)
    _w = jnp.asarray

    def _L0_attn_setup():
        import jax, jax.numpy as jnp
        import numpy as np
        HIDDEN = 1024
        NUM_HEADS = 32
        HEAD_DIM = HIDDEN // NUM_HEADS
        THRESH = 0.001
        key = jax.random.key(seed)
        ks = jax.random.split(key, 9)
        w_std = 0.02
        x = jax.random.normal(ks[0], (4, 1024, HIDDEN), dtype=jnp.float32)
        Wq = jax.random.normal(ks[1], (HIDDEN, HIDDEN), dtype=jnp.float32) * w_std
        bq = jax.random.normal(ks[2], (HIDDEN,), dtype=jnp.float32) * w_std
        Wk = jax.random.normal(ks[3], (HIDDEN, HIDDEN), dtype=jnp.float32) * w_std
        bk = jax.random.normal(ks[4], (HIDDEN,), dtype=jnp.float32) * w_std
        Wv = jax.random.normal(ks[5], (HIDDEN, HIDDEN), dtype=jnp.float32) * w_std
        bv = jax.random.normal(ks[6], (HIDDEN,), dtype=jnp.float32) * w_std
        Wo = jax.random.normal(ks[7], (HIDDEN, HIDDEN), dtype=jnp.float32) * w_std
        bo = jax.random.normal(ks[8], (HIDDEN,), dtype=jnp.float32) * w_std
        return {'x': x, 'Wq': Wq, 'bq': bq, 'Wk': Wk, 'bk': bk, 'Wv': Wv, 'bv': bv, 'Wo': Wo, 'bo': bo}
    _L0_attn_in = _L0_attn_setup()

    def _L0_ffn_setup():
        import jax, jax.numpy as jnp
        import numpy as np
        H = 1024
        I = 3584
        G = 128

        def dequant(q, s, g=G):
            O, In = q.shape
            return (q.reshape(O, In // g, g).astype(s.dtype) * s[:, :, None]).reshape(O, In)
        key = jax.random.key(seed)
        ks = jax.random.split(key, 7)
        x = jax.random.normal(ks[0], (2, 512, H), dtype=jnp.float32)

        def mk_qlinear(kq, ksc, out_d, in_d):
            q = jax.random.randint(kq, (out_d, in_d), -8, 8, dtype=jnp.int32)
            s = jax.random.uniform(ksc, (out_d, in_d // G), dtype=jnp.float32, minval=0.005, maxval=0.02)
            return (q, s)
        gate_q, gate_s = mk_qlinear(ks[1], ks[2], I, H)
        up_q, up_s = mk_qlinear(ks[3], ks[4], I, H)
        down_q, down_s = mk_qlinear(ks[5], ks[6], H, I)
        return {'x': x, 'gate_q': gate_q, 'gate_s': gate_s, 'up_q': up_q, 'up_s': up_s, 'down_q': down_q, 'down_s': down_s}
    _L0_ffn_in = _L0_ffn_setup()
    _d = {'L0_attn_x': _L0_attn_in['x'], 'L0_attn_Wq': _L0_attn_in['Wq'], 'L0_attn_bq': _L0_attn_in['bq'], 'L0_attn_Wk': _L0_attn_in['Wk'], 'L0_attn_bk': _L0_attn_in['bk'], 'L0_attn_Wv': _L0_attn_in['Wv'], 'L0_attn_bv': _L0_attn_in['bv'], 'L0_attn_Wo': _L0_attn_in['Wo'], 'L0_attn_bo': _L0_attn_in['bo'], 'L0_ffn_gate_q': _L0_ffn_in['gate_q'], 'L0_ffn_gate_s': _L0_ffn_in['gate_s'], 'L0_ffn_up_q': _L0_ffn_in['up_q'], 'L0_ffn_up_s': _L0_ffn_in['up_s'], 'L0_ffn_down_q': _L0_ffn_in['down_q'], 'L0_ffn_down_s': _L0_ffn_in['down_s']}
    _x0 = _d['L0_attn_x']
    _d['L0_attn_x'] = jax.random.normal(jax.random.fold_in(jax.random.key(seed), 1), (4, 512, 1024), dtype=_x0.dtype)
    del _x0
    return _d

def reference(L0_attn_x, L0_attn_Wq, L0_attn_bq, L0_attn_Wk, L0_attn_bk, L0_attn_Wv, L0_attn_bv, L0_attn_Wo, L0_attn_bo, L0_ffn_gate_q, L0_ffn_gate_s, L0_ffn_up_q, L0_ffn_up_s, L0_ffn_down_q, L0_ffn_down_s):

    def _L0_attn_ref(x, Wq, bq, Wk, bk, Wv, bv, Wo, bo):
        import jax, jax.numpy as jnp
        import numpy as np
        HIDDEN = 1024
        NUM_HEADS = 32
        HEAD_DIM = HIDDEN // NUM_HEADS
        THRESH = 0.001
        B, S, Hd = x.shape
        H, D = (NUM_HEADS, HEAD_DIM)
        q = (x @ Wq.T + bq).reshape(B, S, H, D)
        k = (x @ Wk.T + bk).reshape(B, S, H, D)
        v = (x @ Wv.T + bv).reshape(B, S, H, D)
        inv_sqrt_d = np.float32(1.0 / np.sqrt(D))
        scores = jnp.einsum('bshd,bsgd->bshg', q, k) * inv_sqrt_d
        scores = jnp.where(scores > THRESH, scores, -jnp.inf)
        attn = jax.nn.softmax(scores, axis=-1)
        out = jnp.einsum('bshg,bsgd->bshd', attn, v).reshape(B, S, Hd)
        return out @ Wo.T + bo

    def _L0_ffn_ref(x, gate_q, gate_s, up_q, up_s, down_q, down_s):
        import jax, jax.numpy as jnp
        import numpy as np
        H = 1024
        I = 3584
        G = 128

        def dequant(q, s, g=G):
            O, In = q.shape
            return (q.reshape(O, In // g, g).astype(s.dtype) * s[:, :, None]).reshape(O, In)
        Wg = dequant(gate_q, gate_s)
        Wu = dequant(up_q, up_s)
        Wd = dequant(down_q, down_s)
        gate_score = jax.nn.silu(jnp.einsum('bsh,ih->bsi', x, Wg))
        intermediate = gate_score * jnp.einsum('bsh,ih->bsi', x, Wu)
        return jnp.einsum('bsi,hi->bsh', intermediate, Wd)
    x = L0_attn_x
    xn = _layernorm(x, axis=-1)
    x = x + _L0_attn_ref(xn, L0_attn_Wq, L0_attn_bq, L0_attn_Wk, L0_attn_bk, L0_attn_Wv, L0_attn_bv, L0_attn_Wo, L0_attn_bo) + _L0_ffn_ref(xn, L0_ffn_gate_q, L0_ffn_gate_s, L0_ffn_up_q, L0_ffn_up_s, L0_ffn_down_q, L0_ffn_down_s)
    return x

_drawn_inputs = setup_inputs


def setup_inputs(seed=0):
    import zlib

    import numpy as np

    out = dict(_drawn_inputs(seed))
    spreads = {}
    factors = {'L0_attn_Wq': 6.413,
     'L0_attn_bq': 8.0,
     'L0_attn_Wk': 6.279,
     'L0_attn_bk': 8.0,
     'L0_attn_Wv': 4.759,
     'L0_attn_bv': 8.0,
     'L0_attn_Wo': 4.758,
     'L0_attn_bo': 38.11}
    for name, (base, spread) in spreads.items():
        noise = np.random.default_rng([zlib.crc32(name.encode()), seed]).standard_normal(out[name].shape)
        drawn = base * np.exp(spread * noise) if base else spread * noise
        out[name] = jnp.asarray(drawn.astype(out[name].dtype))
    for name, factor in factors.items():
        out[name] = (out[name] * factor).astype(out[name].dtype)
    return out
```

```python
from contextlib import ExitStack

import numpy as np

import concourse.bass as bass
from concourse import mybir

F32 = mybir.dt.float32
F16 = mybir.dt.float16
I32 = mybir.dt.int32
ALU = mybir.AluOpType
ACT = mybir.ActivationFunctionType
AX_X = mybir.AxisListType.X

P = 128
HI, LO = 0, 1
BANK = 512


def build(nc, x_in, Wq, bq, Wk, bk, Wv, bv, Wo, bo, gate_q, gate_s, up_q, up_s, down_q, down_s, out):
    B, S, H = x_in.shape
    T = B * S
    KT = H // P
    DH = 32
    NH = H // DH
    TG = P // DH
    GROUPS = P // TG
    INTER = gate_q.shape[0]
    NI = INTER // P
    TT = T // P
    HALF = T // 2
    CHUNK = T // 4
    CT = CHUNK // P
    EPS = 1e-5
    THRESH = 0.001
    INV_SQRT_D = float(np.float32(1.0 / np.sqrt(DH)))
    W_SCALE = 64.0
    W_UNSCALE = 1.0 / W_SCALE
    assert CHUNK == BANK and KT == 8 and gate_s.shape[1] == KT and down_s.shape[1] == NI and NH == 32

    x_rows = x_in.rearrange("b s h -> (b s) h")
    out_rows = out.rearrange("b s h -> (b s) h")
    ctx_dram = nc.dram_tensor("ctx_scratch", [TT, P, 2, KT, P], F16).ap()
    xt_dram = nc.dram_tensor("xt_scratch", [TT, P, 2, KT, P], F16).ap()

    with ExitStack() as whole:
        def sem(name):
            return whole.enter_context(nc.semaphore(name))

        def sb(stack, name, shape, dt):
            return stack.enter_context(nc.sbuf_tensor(name, shape, dt))

        ident32 = sb(whole, "ident32", [P, P], F32)
        ident16 = sb(whole, "ident16", [P, P], F16)
        bias_o = sb(whole, "bias_o", [P, KT], F32)
        psum = whole.enter_context(nc.psum_tensor("banks", [P, 8, BANK], F32))

        with ExitStack() as st:
            wt = sb(st, "wt", [P, 2, 3, KT, H], F16)
            bias_qkv = sb(st, "bias_qkv", [P, 3, H], F32)
            x_tile = sb(st, "x_tile", [P, H], F32)
            xt_tile = sb(st, "xt_tile", [P, 2, 2 * KT * P], F16)
            stats = sb(st, "stats", [P, 2, 6], F32)
            ln_small = sb(st, "ln_small", [P, 8], F32)
            sums = sb(st, "sums", [P, 3, GROUPS], F32)
            with ExitStack() as s1:
                w_rows = sb(s1, "w_rows", [P, 2, H], F32)
            with ExitStack() as s2:
                turned = sb(s2, "turned", [P, 3, P * NH], F16)
                probs_t = sb(s2, "probs_t", [P, GROUPS * P], F16)
                unit32 = sb(s2, "unit32", [P, 2, BANK], F32)
                stacks = sb(s2, "stacks", [P, 3, NH, 4 * DH], F16)
                s_c = sb(s2, "s_c", [P, GROUPS, DH], F32)
                p_c = sb(s2, "p_c", [P, GROUPS, DH], F32)
                p_stack = sb(s2, "p_stack", [P, GROUPS, 4, DH], F16)
                ctx_32 = sb(s2, "ctx_32", [P, KT, P], F32)
                ctx_parts = sb(s2, "ctx_parts", [P, 2, KT, P], F16)

        acc = sb(whole, "acc", [P, KT, T], F32)
        xt = sb(whole, "xt", [P, TT, 2, KT, P], F16)
        gate_scale = sb(whole, "gate_scale", [P, NI, KT], F32)
        up_scale = sb(whole, "up_scale", [P, NI, KT], F32)
        down_scale = sb(whole, "down_scale", [P, KT, NI], F32)
        with ExitStack() as s3:
            wo_t = sb(s3, "wo_t", [P, 2, KT, H], F16)
            wo_rows = sb(s3, "wo_rows", [P, 2, H], F32)
            ctx_t = sb(s3, "ctx_t", [P, 2, CT, 2, KT, P], F16)
        with ExitStack() as s4:
            q_raw = sb(s4, "q_raw", [P, 3, H], I32)
            q_16 = sb(s4, "q_16", [P, 3, H], F16)
            q_t = sb(s4, "q_t", [P, 3, KT, P], F16)
            g_acc = sb(s4, "g_acc", [P, 2, HALF], F32)
            u_acc = sb(s4, "u_acc", [P, 2, HALF], F32)
            h_sb = sb(s4, "h_sb", [P, 2, HALF], F32)
            h_parts = sb(s4, "h_parts", [P, 2, T], F16)
            down_tmp = sb(s4, "down_tmp", [P, 2, HALF], F32)
        with ExitStack() as s5:
            x_res = sb(s5, "x_res", [P, 4, H], F32)
            y_sb = sb(s5, "y_sb", [P, 2, H], F32)

        const_mem = sem("const_mem")
        const_ready = sem("const_ready")
        w_loaded = [sem(f"w_loaded{k}") for k in range(2)]
        w_turned = sem("w_turned")
        w_hi = sem("w_hi")
        w_lo = sem("w_lo")
        bias_loaded = sem("bias_loaded")
        x_loaded = sem("x_loaded")
        ln_stats = sem("ln_stats")
        ln_mv = sem("ln_mv")
        ln_var = sem("ln_var")
        ln_std = sem("ln_std")
        ln_rstd = sem("ln_rstd")
        xn_ready = sem("xn_ready")
        x_turned = sem("x_turned")
        x_hi = sem("x_hi")
        x_lo = sem("x_lo")
        xt_stored = sem("xt_stored")
        unit_done = sem("unit_done")
        unit_copied = sem("unit_copied")
        unit_hi = sem("unit_hi")
        unit_lo = sem("unit_lo")
        batch_done = sem("batch_done")
        batch_out = [sem("batch_out_act"), sem("batch_out_dve")]
        s_done = sem("s_done")
        s_out = sem("s_out")
        row_max = sem("row_max")
        shifted = sem("shifted")
        exp_done = sem("exp_done")
        mask_done = sem("mask_done")
        sum_done = sem("sum_done")
        recip_done = sem("recip_done")
        norm_done = sem("norm_done")
        p_hi = sem("p_hi")
        p_lo = sem("p_lo")
        pv_done = sem("pv_done")
        pv_out = [sem("pv_out_act"), sem("pv_out_dve")]
        ctx_hi = sem("ctx_hi")
        ctx_lo = sem("ctx_lo")
        ctx_stored = sem("ctx_stored")
        scales_loaded = sem("scales_loaded")
        xt_loaded = sem("xt_loaded")
        wo_loaded = [sem(f"wo_loaded{k}") for k in range(2)]
        wo_turned = sem("wo_turned")
        wo_hi = sem("wo_hi")
        wo_lo = sem("wo_lo")
        ctx_loaded = [sem(f"ctx_loaded{k}") for k in range(2)]
        proj_done = sem("proj_done")
        proj_out = sem("proj_out")
        q_loaded = [sem(f"q_loaded{k}") for k in range(3)]
        q_conv = [sem(f"q_conv{k}") for k in range(3)]
        q_turned = [sem(f"q_turned{k}") for k in range(3)]
        q_ready = [sem(f"q_ready{k}") for k in range(3)]
        gu_done = sem("gu_done")
        gu_first = sem("gu_first")
        gu_added = sem("gu_added")
        silu_done = sem("silu_done")
        h_done = sem("h_done")
        h_hi = sem("h_hi")
        h_lo = sem("h_lo")
        down_done = sem("down_done")
        down_copied = sem("down_copied")
        down_added = sem("down_added")
        y_turned = sem("y_turned")
        res_loaded = [sem(f"res_loaded{k}") for k in range(4)]
        y_ready = sem("y_ready")
        y_stored = [sem(f"y_stored{k}") for k in range(2)]

        anchors = sem("anchors")

        def anchor(eng):
            eng.sem_inc(anchors, 1)

        block = whole.enter_context(nc.Block())
        GATE, UP, DOWN = 0, 1, 2
        Q, K, V = 0, 1, 2

        STEPS = [["T0", "T1"], ["T2", "T3"], ["T4", "T5"], ["T6", "T7"], ["S0", "S1"], ["S2", "S3"],
                 ["T8", "T9"], ["T10", "T11"], ["X"], ["T12"], ["T13", "V0", "T14"],
                 ["V1", "T15", "V2", "V3"]]
        HALVES = len(STEPS)

        def walk(eng, body):
            body(0)
            body(1)
            with eng.Fori(2, TT - 1) as i:
                body(i)
            body(TT - 1)
            body(TT)

        def steps_of(i, s):
            for name in STEPS[s]:
                kind, n = name[0], int(name[1:] or 0)
                if kind == "X":
                    if not isinstance(i, int) or i + 1 < TT:
                        yield kind, n
                elif not isinstance(i, int) or i >= 1:
                    yield kind, n

        def projects(i):
            return not (isinstance(i, int) and i == TT)

        def wait_pos(eng, s, value):
            if not isinstance(value, int) or value > 0:
                eng.wait_ge(s, value)

        BATCH_BANK = 2

        def pair(n):
            return psum[:, 4 + 2 * n:6 + 2 * n, :].rearrange("p b c -> p (b c)")

        def batch_bank(m):
            return psum[:, BATCH_BANK + m % 2, :].bitcast(F16)

        def s_pair(k):
            return k % 2

        def v_pair(k):
            return (k + 1) % 2

        def block_copies(j, k, rs, engine_copy, out_sem):
            src = pair(v_pair(k)).rearrange("p (g c) -> p g c", c=P)
            for r in rs:
                for h4 in range(TG):
                    s_ap = src[r * DH:(r + 1) * DH, :, r * DH:(r + 1) * DH]\
                        .rearrange("p g (a h) -> p h a g", h=TG)[:, h4, :, :]
                    d_ap = ctx_32[h4 * DH:(h4 + 1) * DH, :, :]\
                        .rearrange("p a (g r) -> p r a g", r=TG)[:, r, :, 8 * k:8 * k + 8]
                    last = engine_copy(d_ap, s_ap)
            last.then_inc(out_sem, 1)

        def unit_view(u):
            return unit32[:, u % 2, :].rearrange("p (h d) -> p h d", d=DH)

        def stack_view(u, part):
            mat, h0 = u // 2, (u % 2) * (NH // 2)
            places = ((0, 1) if part == HI else (2, 3)) if mat == 0 else ((0, 2) if part == HI else (1, 3))
            if mat < 2:
                return [stacks[:, mat, h0:h0 + NH // 2, n * DH:(n + 1) * DH] for n in places]
            by_dim = stacks[:, mat, :, :].rearrange("p d (n h) -> p n h d", h=DH)
            return [by_dim[:, n, h0:h0 + NH // 2, :] for n in places]

        def batch_dest(eng, j, m):
            if m < 8:
                wait_pos(eng, s_done, j * 4)
            else:
                wait_pos(eng, pv_done, j * 4)
            if m >= 12:
                return probs_t[:, (m - 12) * 8 * P:(m - 11) * 8 * P]
            return turned[:, m // 4, :].rearrange("p (t x) -> p t x", x=NH)[:, :, 8 * (m % 4):8 * (m % 4) + 8]

        def batch_source(m):
            return batch_bank(m) if m >= 12 else batch_bank(m).rearrange("p (x t) -> p t x", t=P)

        DOWN_AFTER = {}
        for d in range(16):
            DOWN_AFTER.setdefault(5 + 27 * d // 16, []).append(d)
        TURN_GATE, TURN_UP, TURN_DOWN = 17, 24, 28
        CONV_GATE, CONV_UP, CONV_DOWN = 7, 11, 22

        def tiles(eng, body):
            body(0, True, False)
            with eng.Fori(1, NI - 1) as t:
                body(t, False, False)
            body(NI - 1, False, True)

        @block.tensor
        def _(pe):
            mm, turn = nc.tensor.matmul, nc.tensor.transpose
            pe.wait_ge(const_ready, 2)

            def turn_rows(rows, loaded, count, n, side, turned, copied_hi, copied_lo, pair):
                pe.wait_ge(loaded, count)
                if n is not None:
                    pe.wait_ge(copied_lo, n)
                    pe.wait_ge(copied_hi, n)
                for k in range(KT):
                    last = turn(psum[:, 2 * pair + k // 4, (k % 4) * P:(k % 4 + 1) * P],
                                rows[:, side, k * P:(k + 1) * P], ident32[:])
                last.then_inc(turned, 1)

            for n in range(2):
                turn_rows(w_rows, w_loaded[n], 16, None, n, w_turned, w_hi, w_lo, n)
            with pe.Fori(1, 3 * KT // 2) as m:
                for n in range(2):
                    turn_rows(w_rows, w_loaded[n], m * 16 + 16, m * 2 + (n - 1), n, w_turned, w_hi, w_lo, n)
            def turn_x(i):
                pe.wait_ge(xn_ready, i + 1)
                if not isinstance(i, int):
                    pe.wait_ge(s_out, (i - 2) * 4 + 3)
                elif i >= 2:
                    pe.wait_ge(s_out, 4 * (i - 2) + 3)
                for k in range(KT):
                    last = turn(pair(0)[:, k * P:(k + 1) * P], x_tile[:, k * P:(k + 1) * P], ident32[:])
                last.then_inc(x_turned, 1)

            def project(i, s):
                u, ks = s // 2, range(4 * (s % 2), 4 * (s % 2) + 4)
                if s == 0:
                    pe.wait_ge(x_lo, i + 1)
                    pe.wait_ge(x_hi, i + 1)
                if s % 2 == 0:
                    wait_pos(pe, unit_copied, i * 6 + (u - 1))
                for k in ks:
                    for n, (wp, xp) in enumerate(((HI, HI), (LO, HI), (HI, LO))):
                        at = (i % 2) * (2 * KT * P) + (xp * KT + k) * P
                        last = mm(psum[:, u % 2, :], xt_tile[:, :, :].rearrange("p a b -> p (a b)")[:, bass.ds(at, P)],
                                  wt[:, wp, u // 2, k, (u % 2) * BANK:(u % 2 + 1) * BANK],
                                  start=(k == 0 and n == 0), stop=(k == KT - 1 and n == 2))
                if s % 2:
                    last.then_inc(unit_done, 1)

            def batch(j, m):
                if m < 12 and m % 4 == 0:
                    pe.wait_ge(unit_lo, j * 6 + (2 * (m // 4) + 2))
                if m >= 12:
                    pe.wait_ge(p_lo, j * 4 + (m - 12 + 1))
                wait_pos(pe, batch_out[m % 2], j * 8 + m // 2)
                for n in range(8):
                    x = 8 * (m % 4) + n
                    src = stacks[:, m // 4, x, :] if m < 12 else p_stack[:, x, :, :].rearrange("p a b -> p (a b)")
                    last = turn(batch_bank(m)[:, n * P:(n + 1) * P], src, ident16[:])
                last.then_inc(batch_done, 1)

            def scores(j, k):
                if k == 0:
                    pe.wait_ge(batch_out[0], j * 8 + 4)
                    pe.wait_ge(batch_out[1], j * 8 + 4)
                    wait_pos(pe, pv_out[0], j * 4)
                    wait_pos(pe, pv_out[1], j * 4)
                elif k >= 2:
                    pe.wait_ge(s_out, j * 4 + (k - 1))
                for n in range(8):
                    at = (8 * k + n) * P
                    last = mm(pair(s_pair(k))[:, n * P:(n + 1) * P], turned[:, Q, at:at + P],
                              turned[:, K, at:at + P], start=True, stop=True)
                last.then_inc(s_done, 1)

            def head_products(j, k):
                if k == 0:
                    pe.wait_ge(batch_out[0], j * 8 + 6)
                    pe.wait_ge(batch_out[1], j * 8 + 6)
                    pe.wait_ge(s_out, j * 4 + 4)
                elif k == 1:
                    if not isinstance(j, int):
                        pe.wait_ge(x_lo, j + 3)
                        pe.wait_ge(x_hi, j + 3)
                    else:
                        pe.wait_ge(x_lo, min(j + 3, TT))
                        pe.wait_ge(x_hi, min(j + 3, TT))
                else:
                    pe.wait_ge(pv_out[0], j * 4 + (k - 1))
                    pe.wait_ge(pv_out[1], j * 4 + (k - 1))
                pe.wait_ge(batch_out[k % 2], j * 8 + (6 + k // 2 + 1))
                for n in range(8):
                    at = (8 * k + n) * P
                    last = mm(pair(v_pair(k))[:, n * P:(n + 1) * P], turned[:, V, at:at + P],
                              probs_t[:, at:at + P], start=True, stop=True)
                last.then_inc(pv_done, 1)

            turn_x(0)
            pe.wait_ge(w_lo, 3 * KT)
            pe.wait_ge(w_hi, 3 * KT)

            def tile_2(i):
                for s in range(HALVES):
                    if projects(i):
                        project(i, s)
                    for kind, n in steps_of(i, s):
                        if kind == "X":
                            turn_x(i + 1)
                        elif kind == "T":
                            batch(i - 1, n)
                        elif kind == "S":
                            scores(i - 1, n)
                        else:
                            head_products(i - 1, n)

            walk(pe, tile_2)

            pe.wait_ge(batch_out[1], TT * 8)
            pe.wait_ge(unit_copied, TT * 6)
            for n in range(KT):
                pe.wait_ge(wo_loaded[n % 2], 16 * (n // 2 + 1))
                if n >= 2:
                    pe.wait_ge(wo_hi, n - 1)
                    pe.wait_ge(wo_lo, n - 1)
                for k in range(KT):
                    last = turn(psum[:, 2 * (n % 2) + k // 4, (k % 4) * P:(k % 4 + 1) * P],
                                wo_rows[:, n % 2, k * P:(k + 1) * P], ident32[:])
                last.then_inc(wo_turned, 1)
            pe.wait_ge(wo_hi, KT)
            pe.wait_ge(wo_lo, KT)
            for c in range(B):
                pe.wait_ge(ctx_loaded[c % 2], 16 * (c // 2 + 1))
                for ho in range(KT):
                    n = c * KT + ho
                    if n >= 4:
                        pe.wait_ge(proj_out, n - 3)
                    for k in range(KT):
                        for m, (wp, cp) in enumerate(((HI, HI), (HI, LO), (LO, HI))):
                            last = mm(psum[:, n % 4, :], wo_t[:, wp, k, ho * P:(ho + 1) * P],
                                      ctx_t[:, c % 2, :, cp, k, :], start=(k == 0 and m == 0),
                                      stop=(k == KT - 1 and m == 2))
                    last.then_inc(proj_done, 1)

            def turn_q(mat, t):
                pe.wait_ge(q_conv[mat], t + 1)
                if mat == GATE:
                    wait_pos(pe, q_ready[DOWN], t - 1)
                if mat == DOWN:
                    pe.wait_ge(q_ready[GATE], min(t + 2, NI) if isinstance(t, int) else t + 2)
                if mat == UP:
                    wait_pos(pe, q_ready[UP], t)
                bank = psum[:, 7 if mat == UP else 6, :].bitcast(F16)
                for k in range(KT):
                    last = turn(bank[:, k * P:(k + 1) * P], q_16[:, mat, k * P:(k + 1) * P], ident16[:])
                last.then_inc(q_turned[mat], 1)

            def gate_up(t, idx):
                mat, g, half = idx // 16, idx // 2 % 8, idx % 2
                if idx in (0, 16):
                    pe.wait_ge(q_ready[mat], t + 1)
                if g == 1:
                    pe.wait_ge(gu_first, t * 4 + (2 * mat + half + 1))
                else:
                    a = (14 * mat + 2 * (g - 2) + half + 1) if g else 14 * mat - 2 + half + 1
                    wait_pos(pe, gu_added, t * 28 + a)
                for c in range(2):
                    for part in (HI, LO):
                        last = mm(psum[:, 2 * half + c, :], q_t[:, mat, g, :],
                                  xt[:, (2 * half + c) * CT:(2 * half + c + 1) * CT, part, g, :],
                                  start=(part == HI), stop=(part == LO))
                last.then_inc(gu_done, 1)

            def down(t, d):
                half, ho = d // 8, d % 8
                if d == 0:
                    pe.wait_ge(q_ready[DOWN], t + 1)
                if ho == 0:
                    pe.wait_ge(h_lo, t * 2 + (half + 1))
                pe.wait_ge(down_copied, t * 16 + (d + 1))
                for c in range(2):
                    for part in (HI, LO):
                        last = mm(psum[:, 4 + c, :], q_t[:, DOWN, ho, :],
                                  h_parts[:, part, half * HALF + c * BANK:half * HALF + (c + 1) * BANK],
                                  start=(part == HI), stop=(part == LO))
                last.then_inc(down_done, 1)

            pe.wait_ge(proj_out, B * KT)
            pe.wait_ge(xt_loaded, 4 * 16)
            turn_q(GATE, 0)
            turn_q(UP, 0)

            def tile(t, first, last):
                for idx in range(32):
                    gate_up(t, idx)
                    if not first:
                        for d in DOWN_AFTER.get(idx, ()):
                            down(t - 1, d)
                    if idx == TURN_GATE and not last:
                        turn_q(GATE, t + 1)
                    if idx == TURN_UP and not last:
                        turn_q(UP, t + 1)
                    if idx == TURN_DOWN:
                        turn_q(DOWN, t)

            tiles(pe, tile)
            for d in range(16):
                down(NI - 1, d)

            def turn_out(u, n, first):
                if not first:
                    pe.wait_ge(y_ready, u - 3)
                for k in range(KT):
                    last = turn(psum[:, 2 * n + k // 4, (k % 4) * P:(k % 4 + 1) * P],
                                acc[:, k, u * P:(u + 1) * P], ident32[:])
                last.then_inc(y_turned, 1)

            pe.wait_ge(down_added, 2 + 16 * NI)
            pe.wait_ge(down_copied, 1 + 16 * NI)
            for u in range(TT):
                turn_out(u, u % 4, u < 4)

        @block.scalar
        def _(act):
            run = nc.scalar.activation

            def pair_of(n):
                return psum[:, 2 * n:2 * n + 2, :].rearrange("p b (k r) -> p (b k) r", r=P)

            def w_dest(part, mat, m, n):
                return wt[:, part, mat, :, bass.ds(m * (2 * P) + n * P, P)]

            for mat in range(3):
                with act.Fori(0, KT // 2) as m:
                    for n in range(2):
                        act.wait_ge(w_turned, m * 2 + (mat * KT + n + 1))
                        run(w_dest(HI, mat, m, n), pair_of(n), ACT.Copy, scale=W_SCALE).then_inc(w_hi, 1)
            def root(i):
                act.wait_ge(ln_var, i + 1)
                run(ln_small[:, 3:4], ln_small[:, 2:3], ACT.Sqrt).then_inc(ln_std, 1)

            def x_part(i):
                act.wait_ge(x_turned, i + 1)
                wait_pos(act, xt_stored, i * 16 - 16)
                wait_pos(act, unit_done, i * 6 - 6)
                flat = xt_tile[:, :, :].rearrange("p a b -> p (a b)")
                run(flat[:, bass.ds((i % 2) * (2 * KT * P), KT * P)], pair(0), ACT.Copy).then_inc(x_hi, 1)

            def unit_part(i, u):
                act.wait_ge(unit_copied, i * 6 + (u + 1))
                wait_pos(act, batch_done, i * 16 - 16 + 4 * (u // 2) + 4)
                dst, src = stack_view(u, HI), unit_view(u)
                for n in range(2):
                    last = run(dst[n], src, ACT.Copy)
                last.then_inc(unit_hi, 1)

            def batch_copy(j, m):
                act.wait_ge(batch_done, j * 16 + (m + 1))
                dst = batch_dest(act, j, m)
                run(dst, batch_source(m), ACT.Copy).then_inc(batch_out[0], 1)

            def scores_out(j, k):
                act.wait_ge(s_done, j * 4 + (k + 1))
                if k == 0:
                    wait_pos(act, mask_done, j)
                src = pair(s_pair(k)).rearrange("p (g c) -> p g c", c=P)
                for r in range(TG):
                    last = run(s_c[r * DH:(r + 1) * DH, 8 * k:8 * k + 8, :],
                               src[r * DH:(r + 1) * DH, :, r * DH:(r + 1) * DH], ACT.Copy, scale=INV_SQRT_D)
                last.then_inc(s_out, 1)

            def exponentials(j):
                act.wait_ge(shifted, j + 1)
                run(p_c[:], p_c[:], ACT.Exp).then_inc(exp_done, 1)

            def prob_hi(j, q):
                if q == 0:
                    act.wait_ge(norm_done, j + 1)
                wait_pos(act, batch_done, j * 16 + (q - 3))
                for n in range(2):
                    last = run(p_stack[:, 8 * q:8 * q + 8, n, :], p_c[:, 8 * q:8 * q + 8, :], ACT.Copy)
                last.then_inc(p_hi, 1)

            def context_hi(j):
                act.wait_ge(pv_out[0], j * 4 + 4)
                act.wait_ge(pv_out[1], j * 4 + 4)
                wait_pos(act, ctx_stored, j * 16)
                run(ctx_parts[:, HI, :, :], ctx_32[:], ACT.Copy).then_inc(ctx_hi, 1)

            def head_copies(j, k):
                act.wait_ge(pv_done, j * 4 + (k + 1))
                if k == 0:
                    wait_pos(act, ctx_lo, j)
                block_copies(j, k, (0, 1), lambda d, s: run(d, s, ACT.Copy), pv_out[0])

            root(0)
            x_part(0)

            def tile_2(i):
                for s in range(HALVES):
                    for kind, n in steps_of(i, s):
                        if kind == "X":
                            x_part(i + 1)
                        elif kind == "T" and n % 2 == 0:
                            batch_copy(i - 1, n)
                        elif kind == "S":
                            scores_out(i - 1, n)
                        elif kind == "V":
                            head_copies(i - 1, n)
                    attends = not isinstance(i, int) or i >= 1
                    if s == 4 and (not isinstance(i, int) or i + 1 < TT):
                        root(i + 1)
                    if s == 6 and attends:
                        exponentials(i - 1)
                    if s == 8 and attends:
                        for q in range(4):
                            prob_hi(i - 1, q)
                    if s % 2 and projects(i):
                        unit_part(i, s // 2)
                    if s == HALVES - 1 and attends:
                        context_hi(i - 1)

            walk(act, tile_2)

            for n in range(KT):
                act.wait_ge(wo_turned, n + 1)
                run(wo_t[:, HI, :, n * P:(n + 1) * P], pair_of(n % 2), ACT.Copy, scale=W_SCALE).then_inc(wo_hi, 1)
            for c in range(B):
                for ho in range(KT):
                    n = c * KT + ho
                    act.wait_ge(proj_done, n + 1)
                    run(acc[:, ho, c * CHUNK:(c + 1) * CHUNK], psum[:, n % 4, :], ACT.Identity,
                        bias=bias_o[:, ho:ho + 1], scale=W_UNSCALE).then_inc(proj_out, 1)

            act.wait_ge(scales_loaded, 3 * 16)
            act.sem_inc(down_copied, 1)

            def conv(mat, t):
                act.wait_ge(q_loaded[mat], t * 16 + 16)
                wait_pos(act, q_turned[mat], t)
                run(q_16[:, mat, :], q_raw[:, mat, :], ACT.Copy).then_inc(q_conv[mat], 1)

            def keep(mat, t):
                act.wait_ge(q_turned[mat], t + 1)
                if mat == GATE:
                    wait_pos(act, gu_done, t * 32 - 16)
                if mat == UP:
                    wait_pos(act, gu_done, t * 32)
                bank = psum[:, 7 if mat == UP else 6, :].bitcast(F16)
                run(q_t[:, mat, :, :].rearrange("p k o -> p (k o)"), bank, ACT.Copy).then_inc(q_ready[mat], 1)

            def slot(half, base=0):
                return psum[:, base + 2 * half:base + 2 * half + 2, :].rearrange("p b c -> p (b c)")

            def first_group(t, mat, half):
                acc_of, scale = (g_acc, gate_scale) if mat == GATE else (u_acc, up_scale)
                act.wait_ge(gu_done, t * 32 + (16 * mat + half + 1))
                if mat == UP:
                    wait_pos(act, h_done, t * 2 + (half - 1))
                else:
                    wait_pos(act, silu_done, t * 2 + (half - 1))
                anchor(act)
                run(acc_of[:, half, :], slot(half), ACT.Copy,
                    scale=scale[:, :, :].rearrange("p t k -> p (t k)")[:, bass.ds(t * KT, 1)]).then_inc(gu_first, 1)

            def silu(t, half):
                act.wait_ge(gu_added, t * 28 + (12 + half + 1))
                wait_pos(act, h_lo, t * 2 + (half - 1))
                wait_pos(act, h_hi, t * 2 + (half - 1))
                run(h_sb[:, half, :], g_acc[:, half, :], ACT.Silu).then_inc(silu_done, 1)

            def hidden_hi(t, half):
                act.wait_ge(h_done, t * 2 + (half + 1))
                run(h_parts[:, HI, half * HALF:(half + 1) * HALF], h_sb[:, half, :], ACT.Copy).then_inc(h_hi, 1)

            def down_copy(t, d):
                act.wait_ge(down_done, t * 16 + (d + 1))
                act.wait_ge(down_added, t * 16 + (d + 1))
                anchor(act)
                run(down_tmp[:, d % 2, :], slot(0, 4), ACT.Copy,
                    scale=down_scale[:, :, :].rearrange("p h t -> p (h t)")[:, bass.ds(t + (d % 8) * NI, 1)])\
                    .then_inc(down_copied, 1)

            conv(GATE, 0)
            conv(UP, 0)
            keep(GATE, 0)
            keep(UP, 0)

            def tile(t, first, last):
                for idx in range(32):
                    if idx in (0, 1, 16, 17):
                        first_group(t, idx // 16, idx % 2)
                    if idx == 1 and not first:
                        keep(DOWN, t - 1)
                        hidden_hi(t - 1, 0)
                        hidden_hi(t - 1, 1)
                        keep(UP, t)
                    if not first:
                        for d in DOWN_AFTER.get(idx, ()):
                            down_copy(t - 1, d)
                    if idx == CONV_GATE and not last:
                        conv(GATE, t + 1)
                    if idx == CONV_UP and not last:
                        conv(UP, t + 1)
                    if idx == CONV_DOWN:
                        conv(DOWN, t)
                    if idx == 18:
                        silu(t, 0)
                        silu(t, 1)
                    if idx == TURN_GATE + 2 and not last:
                        keep(GATE, t + 1)

            tiles(act, tile)
            keep(DOWN, NI - 1)
            hidden_hi(NI - 1, 0)
            hidden_hi(NI - 1, 1)
            for d in range(16):
                down_copy(NI - 1, d)

        @block.vector
        def _(dve):
            v = nc.vector

            def pair_of(n):
                return psum[:, 2 * n:2 * n + 2, :].rearrange("p b (k r) -> p (b k) r", r=P)

            def layer_stats(i):
                dve.wait_ge(x_loaded, i * 16 + 16)
                for c in range(2):
                    v.bn_stats(stats[:, c, :], x_tile[:, c * 512:(c + 1) * 512]).then_inc(ln_stats, 1)
                dve.wait_ge(ln_stats, i * 2 + 2)
                anchor(dve)
                v.bn_aggr(ln_small[:, 0:2], stats[:, :, :]).then_inc(ln_mv, 1)
                dve.wait_ge(ln_mv, i + 1)
                v.tensor_scalar(ln_small[:, 2:3], ln_small[:, 1:2], EPS, None, ALU.add).then_inc(ln_var, 1)

            def layer_norm(i):
                dve.wait_ge(ln_std, i + 1)
                v.reciprocal(ln_small[:, 4:5], ln_small[:, 3:4]).then_inc(ln_rstd, 1)
                dve.wait_ge(ln_rstd, i + 1)
                v.tensor_scalar(x_tile[:], x_tile[:], ln_small[:, 0:1], ln_small[:, 4:5],
                                ALU.subtract, ALU.mult).then_inc(xn_ready, 1)

            def x_part(i):
                flat = xt_tile[:, :, :].rearrange("p a b -> p (a b)")
                dve.wait_ge(x_hi, i + 1)
                v.tensor_tensor(flat[:, bass.ds((i % 2) * (2 * KT * P) + KT * P, KT * P)], pair(0),
                                flat[:, bass.ds((i % 2) * (2 * KT * P), KT * P)], ALU.subtract).then_inc(x_lo, 1)

            layer_stats(0)

            for mat in range(3):
                with dve.Fori(0, KT // 2) as m:
                    for n in range(2):
                        at = bass.ds(m * (2 * P) + n * P, P)
                        dve.wait_ge(w_hi, m * 2 + (mat * KT + n + 1))
                        v.scalar_tensor_tensor(out=wt[:, LO, mat, :, at], in0=pair_of(n), scalar=W_SCALE,
                                               in1=wt[:, HI, mat, :, at], op0=ALU.mult,
                                               op1=ALU.subtract).then_inc(w_lo, 1)

            layer_norm(0)
            x_part(0)
            dve.wait_ge(bias_loaded, 4 * 16)

            def unit_copy(i, u):
                dve.wait_ge(unit_done, i * 6 + (u + 1))
                wait_pos(dve, unit_lo, i * 6 + (u - 1))
                v.scalar_tensor_tensor(out=unit32[:, u % 2, :], in0=psum[:, u % 2, :], scalar=W_UNSCALE,
                                       in1=bias_qkv[:, u // 2, (u % 2) * BANK:(u % 2 + 1) * BANK],
                                       op0=ALU.mult, op1=ALU.add).then_inc(unit_copied, 1)

            def batch_copy(j, m):
                dve.wait_ge(batch_done, j * 16 + (m + 1))
                dst = batch_dest(dve, j, m)
                v.tensor_copy(dst, batch_source(m)).then_inc(batch_out[1], 1)

            def over_heads(ap):
                return ap.rearrange("p (g a) -> p g a", a=1).broadcast_to((P, GROUPS, DH))

            def softmax_shift(j):
                dve.wait_ge(s_out, j * 4 + 4)
                v.tensor_reduce(sums[:, 0, :], s_c[:], AX_X, ALU.max).then_inc(row_max, 1)
                dve.wait_ge(row_max, j + 1)
                wait_pos(dve, p_lo, j * 4)
                v.tensor_tensor(p_c[:], s_c[:], over_heads(sums[:, 0, :]), ALU.subtract).then_inc(shifted, 1)

            def softmax_mask(j):
                dve.wait_ge(exp_done, j + 1)
                v.scalar_tensor_tensor(out=p_c[:], in0=s_c[:], scalar=THRESH, in1=p_c[:],
                                       op0=ALU.is_gt, op1=ALU.mult).then_inc(mask_done, 1)
                dve.wait_ge(mask_done, j + 1)
                v.tensor_reduce(sums[:, 1, :], p_c[:], AX_X, ALU.add).then_inc(sum_done, 1)
                dve.wait_ge(sum_done, j + 1)
                v.reciprocal(sums[:, 2, :], sums[:, 1, :]).then_inc(recip_done, 1)
                dve.wait_ge(recip_done, j + 1)
                v.tensor_tensor(p_c[:], p_c[:], over_heads(sums[:, 2, :]), ALU.mult).then_inc(norm_done, 1)

            def head_copies(j, k):
                dve.wait_ge(pv_done, j * 4 + (k + 1))
                if k == 0:
                    wait_pos(dve, ctx_lo, j)
                block_copies(j, k, (2, 3), lambda d, s: v.tensor_copy(d, s), pv_out[1])

            def tile_2(i):
                attends = not isinstance(i, int) or i >= 1
                more = not isinstance(i, int) or i + 1 < TT
                for s in range(HALVES):
                    if s % 2 and projects(i):
                        unit_copy(i, s // 2)
                    for kind, n in steps_of(i, s):
                        if kind == "X":
                            x_part(i + 1)
                        elif kind == "T" and n % 2:
                            batch_copy(i - 1, n)
                        elif kind == "V":
                            head_copies(i - 1, n)
                    if s == 3 and more:
                        layer_stats(i + 1)
                    if s == 5 and more:
                        layer_norm(i + 1)
                    if s == 5 and attends:
                        softmax_shift(i - 1)
                    if s == 6 and attends:
                        softmax_mask(i - 1)

            walk(dve, tile_2)

            for n in range(KT):
                dve.wait_ge(wo_hi, n + 1)
                v.scalar_tensor_tensor(out=wo_t[:, LO, :, n * P:(n + 1) * P], in0=pair_of(n % 2), scalar=W_SCALE,
                                       in1=wo_t[:, HI, :, n * P:(n + 1) * P], op0=ALU.mult,
                                       op1=ALU.subtract).then_inc(wo_lo, 1)

            dve.wait_ge(scales_loaded, 3 * 16)

            def add_group(t, idx):
                mat, g, half = idx // 16, idx // 2 % 8, idx % 2
                acc_of, scale = (g_acc, gate_scale) if mat == GATE else (u_acc, up_scale)
                before = 14 * mat + 2 * (g - 1) + half
                dve.wait_ge(gu_done, t * 32 + (idx + 1))
                if g == 1:
                    dve.wait_ge(gu_first, t * 4 + (2 * mat + half + 1))
                else:
                    dve.wait_ge(gu_added, t * 28 + (before - 2 + 1))
                v.scalar_tensor_tensor(
                    out=acc_of[:, half, :], in0=psum[:, 2 * half:2 * half + 2, :].rearrange("p b c -> p (b c)"),
                    scalar=scale[:, :, :].rearrange("p t k -> p (t k)")[:, bass.ds(t * KT + g, 1)],
                    in1=acc_of[:, half, :], op0=ALU.mult, op1=ALU.add).then_inc(gu_added, 1)

            def hidden(t, half):
                dve.wait_ge(silu_done, t * 2 + (half + 1))
                dve.wait_ge(gu_added, t * 28 + (26 + half + 1))
                v.tensor_tensor(h_sb[:, half, :], h_sb[:, half, :], u_acc[:, half, :], ALU.mult).then_inc(h_done, 1)

            def hidden_lo(t, half):
                at = slice(half * HALF, (half + 1) * HALF)
                dve.wait_ge(h_hi, t * 2 + (half + 1))
                v.tensor_tensor(h_parts[:, LO, at], h_sb[:, half, :], h_parts[:, HI, at], ALU.subtract)\
                    .then_inc(h_lo, 1)

            def tile(t, first, last):
                for idx in range(32):
                    if idx // 2 % 8:
                        add_group(t, idx)
                    if idx in (3, 4) and not first:
                        hidden_lo(t - 1, idx - 3)
                hidden(t, 0)
                hidden(t, 1)

            tiles(dve, tile)
            hidden_lo(NI - 1, 0)
            hidden_lo(NI - 1, 1)

            def residual(u, n, x_count, y_count):
                dve.wait_ge(y_turned, u + 1)
                dve.wait_ge(res_loaded[n], x_count)
                if y_count is not None:
                    dve.wait_ge(y_stored[n % 2], y_count)
                v.tensor_tensor(y_sb[:, n % 2, :], psum[:, 2 * n:2 * n + 2, :].rearrange("p b c -> p (b c)"),
                                x_res[:, n, :], ALU.add).then_inc(y_ready, 1)

            for n in range(4):
                residual(n, n, 16, None if n < 2 else 16)
            with dve.Fori(1, TT // 4) as m:
                for n in range(4):
                    residual(m * 4 + n, n, m * 16 + 16, m * 32 + 16 * (n // 2))

        @block.gpsimd
        def _(pool):
            g = nc.gpsimd
            g.memset(ident32[:], 0.0).then_inc(const_mem, 1)
            g.memset(ident16[:], 0.0).then_inc(const_mem, 1)
            pool.wait_ge(const_mem, 2)
            for m in (ident32, ident16):
                g.affine_select(out=m[:], in_=m[:], compare_op=ALU.not_equal, fill=1.0, base=0,
                                pattern=[[-1, P]], channel_multiplier=1).then_inc(const_ready, 1)

            def lo_part(dst, src, hi):
                return g.tensor_tensor(dst, src, hi, ALU.subtract)

            def unit_part(i, u):
                pool.wait_ge(unit_hi, i * 6 + (u + 1))
                src, hi = unit_view(u), stack_view(u, HI)
                for n in range(2):
                    last = lo_part(stack_view(u, LO)[n], src, hi[n])
                last.then_inc(unit_lo, 1)

            def prob_lo(j, q):
                pool.wait_ge(p_hi, j * 4 + (q + 1))
                at = slice(8 * q, 8 * q + 8)
                for n in range(2):
                    last = lo_part(p_stack[:, at, 2 + n, :], p_c[:, at, :], p_stack[:, at, n, :])
                last.then_inc(p_lo, 1)

            def context_lo(j):
                pool.wait_ge(ctx_hi, j + 1)
                lo_part(ctx_parts[:, LO, :, :], ctx_32[:], ctx_parts[:, HI, :, :]).then_inc(ctx_lo, 1)

            def tile_2(i):
                attends = not isinstance(i, int) or i >= 1
                for s in range(HALVES):
                    if s == 8 and attends:
                        for q in range(4):
                            prob_lo(i - 1, q)
                    if s % 2 and projects(i):
                        unit_part(i, s // 2)
                    if s == HALVES - 1 and attends:
                        context_lo(i - 1)

            walk(pool, tile_2)

            pool.sem_inc(down_added, 2)

            def add_down(t, d):
                half, ho = d // 8, d % 8
                at = slice(half * HALF, (half + 1) * HALF)
                pool.wait_ge(down_copied, t * 16 + (d + 2))
                pool.wait_ge(down_added, t * 16 + (d + 1))
                g.tensor_tensor(acc[:, ho, at], acc[:, ho, at], down_tmp[:, d % 2, :], ALU.add)\
                    .then_inc(down_added, 1)

            def down_tile(t):
                for d in range(16):
                    add_down(t, d)

            with pool.Fori(0, NI) as t:
                down_tile(t)

        @block.sync
        def _(sp):
            for mat, w in enumerate((Wq, Wk, Wv)):
                def load_w(m, n, first):
                    if not first:
                        sp.wait_ge(w_turned, m * 2 + (mat * KT + n - 1))
                    sp.dma_start(w_rows[:, n, :], w[bass.ds(m * (2 * P) + n * P, P), :]).then_inc(w_loaded[n], 16)

                load_w(0, 0, mat == 0)
                load_w(0, 1, mat == 0)
                if mat == 0:
                    sp.dma_start(x_tile[:], x_rows[0:P, :]).then_inc(x_loaded, 16)
                with sp.Fori(1, KT // 2) as m:
                    load_w(m, 0, False)
                    load_w(m, 1, False)
            for r, b in enumerate((bq, bk, bv)):
                sp.dma_start(bias_qkv[:, r, :], b.rearrange("(a n) -> a n", a=1).broadcast_to((P, H)))\
                    .then_inc(bias_loaded, 16)
            sp.dma_start(bias_o[:], bo.rearrange("(g p) -> p g", p=P),
                         allow_slow_non_contiguous=True).then_inc(bias_loaded, 16)

            def load_x(i):
                sp.wait_ge(x_turned, i)
                sp.dma_start(x_tile[:], x_rows[bass.ds(i * P, P), :]).then_inc(x_loaded, 16)

            def store_xt(i):
                sp.wait_ge(x_lo, i + 1)
                anchor(sp)
                src = xt_tile[:, :, :].rearrange("p a b -> p (a b)")[:, bass.ds((i % 2) * (2 * KT * P), 2 * KT * P)]
                sp.dma_start(xt_dram.rearrange("t p a k c -> t p (a k c)")[bass.ds(i, 1), :, :]
                             .rearrange("t p c -> (t p) c"), src).then_inc(xt_stored, 16)

            def store_context(j):
                sp.wait_ge(ctx_lo, j + 1)
                anchor(sp)
                sp.dma_start(ctx_dram.rearrange("t p a k c -> t p (a k c)")[bass.ds(j, 1), :, :]
                             .rearrange("t p c -> (t p) c"),
                             ctx_parts[:, :, :, :].rearrange("p a k c -> p (a k c)")).then_inc(ctx_stored, 16)

            store_xt(0)

            def tile_2(i):
                if not isinstance(i, int) or i + 1 < TT:
                    load_x(i + 1)
                    store_xt(i + 1)
                if not isinstance(i, int) or i >= 1:
                    store_context(i - 1)

            walk(sp, tile_2)

            sp.wait_ge(ctx_stored, 16 * TT)
            sp.wait_ge(xt_stored, 16 * TT)
            sp.wait_ge(pv_done, 4 * TT)
            for n in range(2):
                sp.dma_start(wo_rows[:, n, :], Wo[n * P:(n + 1) * P, :]).then_inc(wo_loaded[n], 16)

            def load_context(c):
                sp.dma_start(ctx_t[:, c % 2, :, :, :, :].rearrange("p t a k c -> p t (a k c)"),
                             ctx_dram[c * CT:(c + 1) * CT].rearrange("t p a k c -> p t (a k c)"))\
                    .then_inc(ctx_loaded[c % 2], 16)

            load_context(0)
            load_context(1)
            for c in range(4):
                sp.dma_start(xt[:, c * CT:(c + 1) * CT, :, :, :].rearrange("p t a k c -> p t (a k c)"),
                             xt_dram[c * CT:(c + 1) * CT].rearrange("t p a k c -> p t (a k c)"))\
                    .then_inc(xt_loaded, 16)
            for dst, s_in in ((gate_scale, gate_s), (up_scale, up_s)):
                sp.dma_start(dst[:], s_in.rearrange("(t p) g -> p t g", p=P)).then_inc(scales_loaded, 16)
            sp.dma_start(down_scale[:], down_s.rearrange("(h p) t -> p h t", p=P)).then_inc(scales_loaded, 16)
            for n in range(2, KT):
                sp.wait_ge(wo_turned, n - 1)
                sp.dma_start(wo_rows[:, n % 2, :], Wo[n * P:(n + 1) * P, :]).then_inc(wo_loaded[n % 2], 16)
            for c in range(2, B):
                sp.wait_ge(proj_done, KT * (c - 1))
                load_context(c)

            sp.wait_ge(proj_done, KT * B)

            def load_q(mat, t):
                wait_pos(sp, q_conv[mat], t)
                anchor(sp)
                if mat == DOWN:
                    sp.dma_start(q_raw[:, DOWN, :].rearrange("p (h i) -> p h i", i=P),
                                 down_q[:, bass.ds(t * P, P)].rearrange("(h p) i -> p h i", p=P))\
                        .then_inc(q_loaded[mat], 16)
                else:
                    src = gate_q if mat == GATE else up_q
                    sp.dma_start(q_raw[:, mat, :], src[bass.ds(t * P, P), :]).then_inc(q_loaded[mat], 16)

            for mat in (GATE, UP, DOWN):
                load_q(mat, 0)
            with sp.Fori(1, NI) as t:
                for mat in (GATE, UP, DOWN):
                    load_q(mat, t)

            sp.wait_ge(down_copied, 1 + 16 * NI)
            sp.wait_ge(down_added, 2 + 16 * NI)

            def load_res(u, n):
                sp.dma_start(x_res[:, n, :], x_rows[bass.ds(u * P, P), :]).then_inc(res_loaded[n], 16)

            def store(u, n):
                sp.wait_ge(y_ready, u + 1)
                sp.dma_start(out_rows[bass.ds(u * P, P), :], y_sb[:, n % 2, :]).then_inc(y_stored[n % 2], 16)

            for n in range(4):
                load_res(n, n)
            with sp.Fori(0, TT // 4 - 1) as m:
                for n in range(4):
                    store(m * 4 + n, n)
                    load_res(m * 4 + (n + 4), n)
            for n in range(4):
                store(TT - 4 + n, n)
            for n in range(2):
                sp.wait_ge(y_stored[n], 16 * TT // 2)


_INS = ["L0_attn_x", "L0_attn_Wq", "L0_attn_bq", "L0_attn_Wk", "L0_attn_bk", "L0_attn_Wv", "L0_attn_bv",
        "L0_attn_Wo", "L0_attn_bo", "L0_ffn_gate_q", "L0_ffn_gate_s", "L0_ffn_up_q", "L0_ffn_up_s",
        "L0_ffn_down_q", "L0_ffn_down_s"]
_OUTS = [((4, 512, 1024), "float32")]


def kernel(**inputs):
    import numpy as _np
    import concourse.bacc as _bacc
    from concourse import mybir as _mybir
    from concourse.bass_utils import run_bass_kernel_spmd as _run

    nc = _bacc.Bacc("TRN2", target_bir_lowering=False, num_devices=1)
    arrays, args = {}, []
    for name in _INS:
        a = _np.ascontiguousarray(inputs[name])
        arrays[f"in_{name}_dram"] = a
        args.append(nc.dram_tensor(f"in_{name}_dram", a.shape, _mybir.dt.from_np(a.dtype), kind="ExternalInput").ap())
    for i, (shape, dtype) in enumerate(_OUTS):
        dt = _mybir.dt.from_np(_np.dtype(dtype))
        args.append(nc.dram_tensor(f"out_{i}_dram", shape, dt, kind="ExternalOutput").ap())
    build(nc, *args)
    r = _run(nc, [arrays], core_ids=[0])
    got = tuple(r.results[0][f"out_{i}_dram"] for i in range(len(_OUTS)))
    return got[0]
```

```python
from contextlib import ExitStack

import numpy as np

import concourse.bass as bass
from concourse import mybir

F32 = mybir.dt.float32
F16 = mybir.dt.float16
I32 = mybir.dt.int32
ALU = mybir.AluOpType
ACT = mybir.ActivationFunctionType
AX_X = mybir.AxisListType.X

P = 128
HI, LO = 0, 1
BANK = 512


def build(nc, x_in, Wq, bq, Wk, bk, Wv, bv, Wo, bo, gate_q, gate_s, up_q, up_s, down_q, down_s, out):
    B, S, H = x_in.shape
    T = B * S
    KT = H // P
    DH = 32
    NH = H // DH
    TG = P // DH
    GROUPS = P // TG
    INTER = gate_q.shape[0]
    NI = INTER // P
    TT = T // P
    HALF = T // 2
    CHUNK = T // 4
    CT = CHUNK // P
    EPS = 1e-5
    THRESH = 0.001
    INV_SQRT_D = float(np.float32(1.0 / np.sqrt(DH)))
    W_SCALE = 64.0
    W_UNSCALE = 1.0 / W_SCALE
    assert CHUNK == BANK and KT == 8 and gate_s.shape[1] == KT and down_s.shape[1] == NI and NH == 32

    x_rows = x_in.rearrange("b s h -> (b s) h")
    out_rows = out.rearrange("b s h -> (b s) h")
    ctx_dram = nc.dram_tensor("ctx_scratch", [TT, P, 2, KT, P], F16).ap()
    xt_dram = nc.dram_tensor("xt_scratch", [TT, P, 2, KT, P], F16).ap()

    with ExitStack() as whole:
        def sem(name):
            return whole.enter_context(nc.semaphore(name))

        def sb(stack, name, shape, dt):
            return stack.enter_context(nc.sbuf_tensor(name, shape, dt))

        ident32 = sb(whole, "ident32", [P, P], F32)
        ident16 = sb(whole, "ident16", [P, P], F16)
        bias_o = sb(whole, "bias_o", [P, KT], F32)
        psum = whole.enter_context(nc.psum_tensor("banks", [P, 8, BANK], F32))

        with ExitStack() as st:
            wt = sb(st, "wt", [P, 2, 3, KT, H], F16)
            bias_qkv = sb(st, "bias_qkv", [P, 3, H], F32)
            x_tile = sb(st, "x_tile", [P, H], F32)
            xt_tile = sb(st, "xt_tile", [P, 2, 2 * KT * P], F16)
            unit32 = sb(st, "unit32", [P, 2, BANK], F32)
            stats = sb(st, "stats", [P, 2, 6], F32)
            ln_small = sb(st, "ln_small", [P, 8], F32)
            sums = sb(st, "sums", [P, 3, GROUPS], F32)
            with ExitStack() as s1:
                w_rows = sb(s1, "w_rows", [P, 4, H], F32)
            with ExitStack() as s2:
                turned = sb(s2, "turned", [P, 3, P * NH], F16)
                probs_t = sb(s2, "probs_t", [P, GROUPS * P], F16)
                stacks = sb(s2, "stacks", [P, 3, NH, 4 * DH], F16)
                s_c = sb(s2, "s_c", [P, GROUPS, DH], F32)
                p_c = sb(s2, "p_c", [P, GROUPS, DH], F32)
                p_stack = sb(s2, "p_stack", [P, GROUPS, 4, DH], F16)
                ctx_32 = sb(s2, "ctx_32", [P, KT, P], F32)
                ctx_parts = sb(s2, "ctx_parts", [P, 2, KT, P], F16)

        LOWER = 72 * 1024
        lower = sb(whole, "lower", [P, LOWER // 4], F32)
        acc = sb(whole, "acc", [P, 2, KT, HALF], F32)
        xt = sb(whole, "xt", [P, TT, 2, KT, P], F16)
        gate_scale = sb(whole, "gate_scale", [P, NI, KT], F32)
        up_scale = sb(whole, "up_scale", [P, NI, KT], F32)
        down_scale = sb(whole, "down_scale", [P, KT, NI], F32)

        def carve(*wanted):
            at, views = 0, []
            for shape, dt in wanted:
                n = int(np.prod(shape))
                words = n // 2 if dt == F16 else n
                view = lower[:, at:at + words]
                view = view if dt == F32 else view.bitcast(dt)
                names = "abcde"[:len(shape)]
                views.append(view.rearrange(f"p ({' '.join(names)}) -> p {' '.join(names)}",
                                            **dict(zip(names[1:], shape[1:]))))
                at += words
            assert at * 4 <= LOWER
            return views

        wo_t, wo_rows, ctx_t = carve(((2, KT, H), F16), ((2, H), F32), ((2, CT, 2, KT, P), F16))
        q_raw, q_16, q_t, g_acc, u_acc, h_sb, h_parts, down_tmp = carve(
            ((3, H), I32), ((3, H), F16), ((3, KT, P), F16), ((2, HALF), F32), ((2, HALF), F32),
            ((2, HALF), F32), ((2, 2, 2, HALF), F16), ((2, HALF), F32))
        x_res, = carve(((4, H), F32))

        const_mem = sem("const_mem")
        const_ready = sem("const_ready")
        w_loaded = [sem(f"w_loaded{k}") for k in range(4)]
        w_turned = sem("w_turned")
        w_hi = sem("w_hi")
        w_lo = sem("w_lo")
        bias_loaded = sem("bias_loaded")
        x_loaded = sem("x_loaded")
        ln_stats = sem("ln_stats")
        ln_mv = sem("ln_mv")
        ln_var = sem("ln_var")
        ln_std = sem("ln_std")
        ln_rstd = sem("ln_rstd")
        xn_ready = sem("xn_ready")
        x_turned = sem("x_turned")
        x_hi = sem("x_hi")
        x_lo = sem("x_lo")
        xt_stored = sem("xt_stored")
        unit_done = sem("unit_done")
        unit_copied = sem("unit_copied")
        unit_hi = sem("unit_hi")
        unit_lo = sem("unit_lo")
        batch_done = sem("batch_done")
        batch_out = [sem("batch_out_act"), sem("batch_out_dve")]
        s_done = sem("s_done")
        s_out = sem("s_out")
        row_max = sem("row_max")
        shifted = sem("shifted")
        exp_done = sem("exp_done")
        mask_done = sem("mask_done")
        sum_done = sem("sum_done")
        recip_done = sem("recip_done")
        norm_done = sem("norm_done")
        p_hi = sem("p_hi")
        p_lo = sem("p_lo")
        pv_done = sem("pv_done")
        pv_out = [sem("pv_out_act"), sem("pv_out_dve")]
        ctx_hi = sem("ctx_hi")
        ctx_lo = sem("ctx_lo")
        ctx_stored = sem("ctx_stored")
        scales_loaded = sem("scales_loaded")
        xt_loaded = sem("xt_loaded")
        wo_loaded = [sem(f"wo_loaded{k}") for k in range(2)]
        wo_turned = sem("wo_turned")
        wo_hi = sem("wo_hi")
        wo_lo = sem("wo_lo")
        ctx_loaded = [sem(f"ctx_loaded{k}") for k in range(2)]
        proj_done = sem("proj_done")
        proj_out = sem("proj_out")
        q_loaded = [sem(f"q_loaded{k}") for k in range(3)]
        q_conv = [sem(f"q_conv{k}") for k in range(3)]
        q_turned = [sem(f"q_turned{k}") for k in range(3)]
        q_ready = [sem(f"q_ready{k}") for k in range(3)]
        gu_done = sem("gu_done")
        gu_first = sem("gu_first")
        gu_added = sem("gu_added")
        silu_done = sem("silu_done")
        h_done = sem("h_done")
        h_hi = sem("h_hi")
        h_lo = sem("h_lo")
        down_done = sem("down_done")
        down_copied = sem("down_copied")
        down_added = sem("down_added")
        tail_done = sem("tail_done")
        tail_added = sem("tail_added")
        y_turned = sem("y_turned")
        res_loaded = [sem(f"res_loaded{k}") for k in range(4)]
        y_ready = sem("y_ready")
        y_stored = [sem(f"y_stored{k}") for k in range(4)]

        anchors = sem("anchors")

        def anchor(eng):
            eng.sem_inc(anchors, 1)

        block = whole.enter_context(nc.Block())
        GATE, UP, DOWN = 0, 1, 2
        Q, K, V = 0, 1, 2

        STEPS = [["T0"], ["T1"], ["T2"], ["T3"], ["T4"], ["T5"], ["T6"], ["T7"], ["T8"], ["S0"], ["S1"],
                 ["T9"], ["S2"], ["S3"], ["T10"], ["T11"], ["X"], [], [], ["T12"], ["T13", "V0"],
                 ["T14", "V1"], ["T15", "V2"], ["V3"]]
        QUARTERS = len(STEPS)
        STATS_AT, ROOT_AT, NORM_AT, SHIFT_AT, EXP_AT, MASK_AT, P_AT = 6, 8, 10, 13, 14, 15, 17
        LAST_UNITS = (QUARTERS - KT) // 2

        def walk(eng, first, body):
            first()
            body(1)
            with eng.Fori(2, TT - 1) as i:
                body(i)
            body(TT - 1)
            body(TT)

        def opening(weights, first_x, unit, next_x):
            weights(0)
            first_x()
            for w in range(1, 6):
                weights(w)
                unit(w - 1)
            unit(5)
            next_x()

        def steps_of(i, s):
            for name in STEPS[s]:
                kind, n = name[0], int(name[1:] or 0)
                if kind == "X":
                    if not isinstance(i, int) or i + 1 < TT:
                        yield kind, n
                else:
                    yield kind, n

        def projects(i):
            return not (isinstance(i, int) and i == TT)

        def wait_pos(eng, s, value):
            if not isinstance(value, int) or value > 0:
                eng.wait_ge(s, value)

        BATCH_BANK = 2

        def pair(n):
            return psum[:, 4 + 2 * n:6 + 2 * n, :].rearrange("p b c -> p (b c)")

        def batch_bank(m):
            return psum[:, BATCH_BANK + m % 2, :].bitcast(F16)

        def s_pair(k):
            return k % 2

        def v_pair(k):
            return (k + 1) % 2

        def block_copies(j, k, rs, engine_copy, out_sem):
            src = pair(v_pair(k)).rearrange("p (g c) -> p g c", c=P)
            for r in rs:
                for h4 in range(TG):
                    s_ap = src[r * DH:(r + 1) * DH, :, r * DH:(r + 1) * DH]\
                        .rearrange("p g (a h) -> p h a g", h=TG)[:, h4, :, :]
                    d_ap = ctx_32[h4 * DH:(h4 + 1) * DH, :, :]\
                        .rearrange("p a (g r) -> p r a g", r=TG)[:, r, :, 8 * k:8 * k + 8]
                    last = engine_copy(d_ap, s_ap)
            last.then_inc(out_sem, 1)

        def unit_view(u):
            return unit32[:, u % 2, :].rearrange("p (h d) -> p h d", d=DH)

        def stack_view(u, part):
            mat, h0 = u // 2, (u % 2) * (NH // 2)
            places = ((0, 1) if part == HI else (2, 3)) if mat == 0 else ((0, 2) if part == HI else (1, 3))
            if mat < 2:
                return [stacks[:, mat, h0:h0 + NH // 2, n * DH:(n + 1) * DH] for n in places]
            by_dim = stacks[:, mat, :, :].rearrange("p d (n h) -> p n h d", h=DH)
            return [by_dim[:, n, h0:h0 + NH // 2, :] for n in places]

        def batch_dest(eng, j, m):
            if m < 8:
                wait_pos(eng, s_done, j * 4)
            else:
                wait_pos(eng, pv_done, j * 4)
            if m >= 12:
                return probs_t[:, (m - 12) * 8 * P:(m - 11) * 8 * P]
            return turned[:, m // 4, :].rearrange("p (t x) -> p t x", x=NH)[:, :, 8 * (m % 4):8 * (m % 4) + 8]

        def batch_source(m):
            return batch_bank(m) if m >= 12 else batch_bank(m).rearrange("p (x t) -> p t x", t=P)

        FIRST_DOWN, EARLY = 18, 7

        def downs(t, idx):
            if idx % 2:
                return
            if idx >= FIRST_DOWN and has_prev(t):
                yield 1, (idx - FIRST_DOWN) // 2
            if idx < FIRST_DOWN and not (isinstance(t, int) and t < 2):
                yield 2, EARLY + idx // 2

        def has_prev(t):
            return not (isinstance(t, int) and t == 0)

        def has_next(t):
            return not (isinstance(t, int) and t == NI - 1)

        TAIL_FROM = 16 * (NI - 2) + EARLY
        TAIL = [(t, d, d % 3 == 0) for t, ds in ((NI - 2, range(EARLY, 16)), (NI - 1, range(16))) for d in ds]
        TAIL_POOL = [(t, d) for t, d, by_pool in TAIL if by_pool]
        TURN_DOWN, TURN_GATE, TURN_UP = 10, 19, 25
        CONV_DOWN, CONV_GATE, CONV_UP = 5, 13, 21
        h_flat = h_parts.rearrange("p a b c d -> p (a b c d)")

        def h_part(t, half, part):
            return h_flat[:, bass.ds((t % 2) * (4 * HALF) + (half * 2 + part) * HALF, HALF)]

        def tiles(eng, body):
            body(0)
            body(1)
            with eng.Fori(2, NI - 1) as t:
                body(t)
            body(NI - 1)

        @block.tensor
        def _(pe):
            mm, turn = nc.tensor.matmul, nc.tensor.transpose
            pe.wait_ge(const_ready, 2)

            def weights(w4):
                for w in range(4 * w4, 4 * w4 + 4):
                    pe.wait_ge(w_loaded[w % 4], 16 * (w4 + 1))
                    if w >= 2:
                        pe.wait_ge(w_hi, w - 1)
                        pe.wait_ge(w_lo, w - 1)
                    if w == 4:
                        pe.wait_ge(x_hi, 1)
                        pe.wait_ge(x_lo, 1)
                    for k in range(KT):
                        last = turn(pair(w % 2)[:, k * P:(k + 1) * P], w_rows[:, w % 4, k * P:(k + 1) * P],
                                    ident32[:])
                    last.then_inc(w_turned, 1)

            def turn_x(i):
                pe.wait_ge(xn_ready, i + 1)
                if isinstance(i, int) and i == 0:
                    pe.wait_ge(w_hi, 3)
                    pe.wait_ge(w_lo, 3)
                elif isinstance(i, int) and i == 1:
                    pe.wait_ge(w_hi, 3 * KT)
                    pe.wait_ge(w_lo, 3 * KT)
                else:
                    pe.wait_ge(s_out, (i - 2) * 4 + 3)
                for k in range(KT):
                    last = turn(pair(0)[:, k * P:(k + 1) * P], x_tile[:, k * P:(k + 1) * P], ident32[:])
                last.then_inc(x_turned, 1)

            def project(i, s):
                u, ks = s // 4, range(2 * (s % 4), 2 * (s % 4) + 2)
                if s == 0:
                    pe.wait_ge(x_lo, i + 1)
                    pe.wait_ge(x_hi, i + 1)
                if s % 4 == 0:
                    wait_pos(pe, unit_copied, i * 6 + (u - 1))
                for k in ks:
                    for n, (wp, xp) in enumerate(((HI, HI), (LO, HI), (HI, LO))):
                        at = (i % 2) * (2 * KT * P) + (xp * KT + k) * P
                        last = mm(psum[:, u % 2, :], xt_tile[:, :, :].rearrange("p a b -> p (a b)")[:, bass.ds(at, P)],
                                  wt[:, wp, u // 2, k, (u % 2) * BANK:(u % 2 + 1) * BANK],
                                  start=(k == 0 and n == 0), stop=(k == KT - 1 and n == 2))
                if s % 4 == 3:
                    last.then_inc(unit_done, 1)

            def batch(j, m):
                if m < 12 and m % 4 == 0:
                    pe.wait_ge(unit_lo, j * 6 + (2 * (m // 4) + 2))
                if m >= 12:
                    pe.wait_ge(p_lo, j * 4 + (m - 12 + 1))
                wait_pos(pe, batch_out[m % 2], j * 8 + m // 2)
                for n in range(8):
                    x = 8 * (m % 4) + n
                    src = stacks[:, m // 4, x, :] if m < 12 else p_stack[:, x, :, :].rearrange("p a b -> p (a b)")
                    last = turn(batch_bank(m)[:, n * P:(n + 1) * P], src, ident16[:])
                last.then_inc(batch_done, 1)

            def scores(j, k):
                if k == 0:
                    pe.wait_ge(batch_out[0], j * 8 + 4)
                    pe.wait_ge(batch_out[1], j * 8 + 4)
                    wait_pos(pe, pv_out[0], j * 4)
                    wait_pos(pe, pv_out[1], j * 4)
                elif k >= 2:
                    pe.wait_ge(s_out, j * 4 + (k - 1))
                for n in range(8):
                    at = (8 * k + n) * P
                    last = mm(pair(s_pair(k))[:, n * P:(n + 1) * P], turned[:, Q, at:at + P],
                              turned[:, K, at:at + P], start=True, stop=True)
                last.then_inc(s_done, 1)

            def head_products(j, k):
                if k == 0:
                    pe.wait_ge(batch_out[0], j * 8 + 6)
                    pe.wait_ge(batch_out[1], j * 8 + 6)
                    pe.wait_ge(s_out, j * 4 + 4)
                elif k == 1:
                    if not isinstance(j, int):
                        pe.wait_ge(x_lo, j + 3)
                        pe.wait_ge(x_hi, j + 3)
                    else:
                        pe.wait_ge(x_lo, min(j + 3, TT))
                        pe.wait_ge(x_hi, min(j + 3, TT))
                else:
                    pe.wait_ge(pv_out[0], j * 4 + (k - 1))
                    pe.wait_ge(pv_out[1], j * 4 + (k - 1))
                pe.wait_ge(batch_out[k % 2], j * 8 + (6 + k // 2 + 1))
                for n in range(8):
                    at = (8 * k + n) * P
                    last = mm(pair(v_pair(k))[:, n * P:(n + 1) * P], turned[:, V, at:at + P],
                              probs_t[:, at:at + P], start=True, stop=True)
                last.then_inc(pv_done, 1)

            def first_unit(u):
                pe.wait_ge(w_hi, 4 * u + 4)
                pe.wait_ge(w_lo, 4 * u + 4)
                for s in range(4 * u, 4 * u + 4):
                    project(0, s)

            def turn_wo(n):
                pe.wait_ge(wo_loaded[n % 2], 16 * (n // 2 + 1))
                if n == 0:
                    pe.wait_ge(unit_copied, TT * 6)
                else:
                    pe.wait_ge(wo_hi, n)
                    pe.wait_ge(wo_lo, n)
                for k in range(KT):
                    last = turn(psum[:, k // 4, (k % 4) * P:(k % 4 + 1) * P],
                                wo_rows[:, n % 2, k * P:(k + 1) * P], ident32[:])
                last.then_inc(wo_turned, 1)

            def output_unit(n, ks):
                c, ho = n // KT, n % KT
                if ks[0] == 0:
                    if n == 0:
                        pe.wait_ge(wo_hi, KT)
                        pe.wait_ge(wo_lo, KT)
                    if ho == 0:
                        pe.wait_ge(ctx_loaded[c % 2], 16 * (c // 2 + 1))
                    if n >= 2:
                        pe.wait_ge(proj_out, n - 1)
                for k in ks:
                    for m, (wp, cp) in enumerate(((HI, HI), (HI, LO), (LO, HI))):
                        last = mm(psum[:, n % 2, :], wo_t[:, wp, k, ho * P:(ho + 1) * P],
                                  ctx_t[:, c % 2, :, cp, k, :], start=(k == 0 and m == 0),
                                  stop=(k == KT - 1 and m == 2))
                if ks[-1] == KT - 1:
                    last.then_inc(proj_done, 1)

            def tile_2(i):
                for s in range(QUARTERS):
                    if projects(i):
                        project(i, s)
                    elif s < KT:
                        turn_wo(s)
                    else:
                        half = (s - KT) % 2
                        output_unit((s - KT) // 2, range(4 * half, 4 * half + 4))
                    for kind, n in steps_of(i, s):
                        if kind == "X":
                            turn_x(i + 1)
                        elif kind == "T":
                            batch(i - 1, n)
                        elif kind == "S":
                            scores(i - 1, n)
                        else:
                            head_products(i - 1, n)

            walk(pe, lambda: opening(weights, lambda: turn_x(0), first_unit, lambda: turn_x(1)), tile_2)

            for n in range(LAST_UNITS, 4 * KT):
                output_unit(n, range(KT))

            def turn_q(mat, t):
                pe.wait_ge(q_conv[mat], t + 1)
                if mat == GATE:
                    wait_pos(pe, q_ready[DOWN], t - 1)
                if mat == DOWN:
                    pe.wait_ge(q_ready[GATE], min(t + 2, NI) if isinstance(t, int) else t + 2)
                if mat == UP:
                    wait_pos(pe, q_ready[UP], t)
                bank = psum[:, 7 if mat == UP else 6, :].bitcast(F16)
                for k in range(KT):
                    last = turn(bank[:, k * P:(k + 1) * P], q_16[:, mat, k * P:(k + 1) * P], ident16[:])
                last.then_inc(q_turned[mat], 1)

            def gate_up(t, idx):
                mat, g, half = idx // 16, idx // 2 % 8, idx % 2
                if idx in (0, 16):
                    pe.wait_ge(q_ready[mat], t + 1)
                if g == 1:
                    pe.wait_ge(gu_first, t * 4 + (2 * mat + half + 1))
                else:
                    a = (14 * mat + 2 * (g - 2) + half + 1) if g else 14 * mat - 2 + half + 1
                    wait_pos(pe, gu_added, t * 28 + a)
                for c in range(2):
                    for part in (HI, LO):
                        last = mm(psum[:, 2 * half + c, :], q_t[:, mat, g, :],
                                  xt[:, (2 * half + c) * CT:(2 * half + c + 1) * CT, part, g, :],
                                  start=(part == HI), stop=(part == LO))
                last.then_inc(gu_done, 1)

            def down_into(bank, t, d, done):
                half, ho = d // 8, d % 8
                if d == 0:
                    pe.wait_ge(q_ready[DOWN], t + 1)
                if ho == 0:
                    pe.wait_ge(h_lo, t * 2 + (half + 1))
                for c in range(2):
                    for part in (HI, LO):
                        at = (t % 2) * (4 * HALF) + ((half * 2 + part) * HALF + c * BANK)
                        last = mm(psum[:, bank + c, :], q_t[:, DOWN, ho, :], h_flat[:, bass.ds(at, BANK)],
                                  start=(part == HI), stop=(part == LO))
                last.then_inc(done, 1)

            def down(t, d):
                pe.wait_ge(down_copied, t * 16 + (d + 1))
                down_into(4, t, d, down_done)

            pe.wait_ge(proj_out, 4 * KT)
            pe.wait_ge(xt_loaded, 4 * 16)
            turn_q(GATE, 0)
            turn_q(UP, 0)

            def tile(t):
                for idx in range(32):
                    gate_up(t, idx)
                    for back, d in downs(t, idx):
                        down(t - back, d)
                    if idx == TURN_GATE and has_next(t):
                        turn_q(GATE, t + 1)
                    if idx == TURN_UP and has_next(t):
                        turn_q(UP, t + 1)
                    if idx == TURN_DOWN and has_prev(t):
                        turn_q(DOWN, t - 1)

            tiles(pe, tile)
            turn_q(DOWN, NI - 1)
            fast = 0
            for t, d, by_pool in TAIL:
                if by_pool:
                    n = TAIL_POOL.index((t, d))
                    pe.wait_ge(down_copied, TAIL_FROM + n + 1)
                    down_into(4, t, d, down_done)
                else:
                    if fast < 2:
                        pe.wait_ge(gu_added, NI * 28 - 1 + fast)
                    else:
                        pe.wait_ge(tail_added, fast - 1)
                    down_into(2 * (fast % 2), t, d, tail_done)
                    fast += 1

            def turn_out(u, n, first):
                if not first:
                    pe.wait_ge(y_ready, u - 3)
                for k in range(KT):
                    last = turn(psum[:, 2 * n + k // 4, (k % 4) * P:(k % 4 + 1) * P],
                                acc[:, u // 8, k, (u % 8) * P:(u % 8 + 1) * P], ident32[:])
                last.then_inc(y_turned, 1)

            pe.wait_ge(down_added, 2 + TAIL_FROM + len(TAIL_POOL))
            pe.wait_ge(tail_added, len(TAIL) - len(TAIL_POOL))
            for u in range(TT):
                turn_out(u, u % 4, u < 4)

        @block.scalar
        def _(act):
            run = nc.scalar.activation

            def pair_of(n):
                return pair(n).rearrange("p (k r) -> p k r", r=P)

            def weights(w4):
                for w in range(4 * w4, 4 * w4 + 4):
                    act.wait_ge(w_turned, w + 1)
                    run(wt[:, HI, w // KT, :, (w % KT) * P:(w % KT + 1) * P], pair_of(w % 2), ACT.Copy,
                        scale=W_SCALE).then_inc(w_hi, 1)

            def root(i):
                act.wait_ge(ln_var, i + 1)
                run(ln_small[:, 3:4], ln_small[:, 2:3], ACT.Sqrt).then_inc(ln_std, 1)

            def x_part(i):
                act.wait_ge(x_turned, i + 1)
                wait_pos(act, xt_stored, i * 16 - 16)
                wait_pos(act, unit_done, i * 6 - 6)
                flat = xt_tile[:, :, :].rearrange("p a b -> p (a b)")
                run(flat[:, bass.ds((i % 2) * (2 * KT * P), KT * P)], pair(0), ACT.Copy).then_inc(x_hi, 1)

            def unit_part(i, u):
                act.wait_ge(unit_copied, i * 6 + (u + 1))
                if not isinstance(i, int) or i:
                    act.wait_ge(batch_done, i * 16 + (4 * (u // 2) - 12))
                dst, src = stack_view(u, HI), unit_view(u)
                for n in range(2):
                    last = run(dst[n], src, ACT.Copy)
                last.then_inc(unit_hi, 1)

            def batch_copy(j, m):
                act.wait_ge(batch_done, j * 16 + (m + 1))
                dst = batch_dest(act, j, m)
                run(dst, batch_source(m), ACT.Copy).then_inc(batch_out[0], 1)

            def scores_out(j, k):
                act.wait_ge(s_done, j * 4 + (k + 1))
                if k == 0:
                    wait_pos(act, mask_done, j)
                src = pair(s_pair(k)).rearrange("p (g c) -> p g c", c=P)
                for r in range(TG):
                    last = run(s_c[r * DH:(r + 1) * DH, 8 * k:8 * k + 8, :],
                               src[r * DH:(r + 1) * DH, :, r * DH:(r + 1) * DH], ACT.Copy, scale=INV_SQRT_D)
                last.then_inc(s_out, 1)

            def exponentials(j):
                act.wait_ge(shifted, j + 1)
                run(p_c[:], p_c[:], ACT.Exp).then_inc(exp_done, 1)

            def prob_hi(j, q):
                if q == 0:
                    act.wait_ge(norm_done, j + 1)
                wait_pos(act, batch_done, j * 16 + (q - 3))
                for n in range(2):
                    last = run(p_stack[:, 8 * q:8 * q + 8, n, :], p_c[:, 8 * q:8 * q + 8, :], ACT.Copy)
                last.then_inc(p_hi, 1)

            def context_hi(j):
                act.wait_ge(pv_out[0], j * 4 + 4)
                act.wait_ge(pv_out[1], j * 4 + 4)
                wait_pos(act, ctx_stored, j * 16)
                run(ctx_parts[:, HI, :, :], ctx_32[:], ACT.Copy).then_inc(ctx_hi, 1)

            def head_copies(j, k):
                act.wait_ge(pv_done, j * 4 + (k + 1))
                if k == 0:
                    wait_pos(act, ctx_lo, j)
                block_copies(j, k, (0, 1), lambda d, s: run(d, s, ACT.Copy), pv_out[0])

            def wo_part(n):
                act.wait_ge(wo_turned, n + 1)
                if n == 0:
                    act.wait_ge(unit_done, 6 * TT)
                run(wo_t[:, HI, :, n * P:(n + 1) * P], psum[:, 0:2, :].rearrange("p b (k r) -> p (b k) r", r=P),
                    ACT.Copy, scale=W_SCALE).then_inc(wo_hi, 1)

            def output_out(n):
                c, ho = n // KT, n % KT
                act.wait_ge(proj_done, n + 1)
                run(acc[:, c // 2, ho, (c % 2) * CHUNK:(c % 2 + 1) * CHUNK], psum[:, n % 2, :], ACT.Identity,
                    bias=bias_o[:, ho:ho + 1], scale=W_UNSCALE).then_inc(proj_out, 1)

            def tile_2(i):
                for s in range(QUARTERS):
                    if not projects(i) and s < KT:
                        wo_part(s)
                    for kind, n in steps_of(i, s):
                        if kind == "X":
                            x_part(i + 1)
                        elif kind == "T" and n % 2 == 0:
                            batch_copy(i - 1, n)
                        elif kind == "S":
                            scores_out(i - 1, n)
                        elif kind == "V":
                            head_copies(i - 1, n)
                    if s == ROOT_AT and (not isinstance(i, int) or i + 1 < TT):
                        root(i + 1)
                    if s == EXP_AT:
                        exponentials(i - 1)
                    if s == P_AT:
                        for q in range(4):
                            prob_hi(i - 1, q)
                    if s % 4 == 3 and projects(i):
                        unit_part(i, s // 4)
                    if not projects(i) and s > KT and (s - KT) % 2:
                        output_out((s - KT) // 2)
                context_hi(i - 1)

            root(0)

            def next_x():
                root(1)
                x_part(1)

            walk(act, lambda: opening(weights, lambda: x_part(0), lambda u: unit_part(0, u), next_x), tile_2)

            act.wait_ge(xt_stored, 16 * TT)
            act.wait_ge(ctx_lo, TT)
            for n in range(LAST_UNITS, 4 * KT):
                output_out(n)

            act.wait_ge(scales_loaded, 3 * 16)
            act.sem_inc(down_copied, 1)

            def conv(mat, t):
                act.wait_ge(q_loaded[mat], t * 16 + 16)
                wait_pos(act, q_turned[mat], t)
                run(q_16[:, mat, :], q_raw[:, mat, :], ACT.Copy).then_inc(q_conv[mat], 1)

            def keep(mat, t):
                act.wait_ge(q_turned[mat], t + 1)
                if mat == GATE:
                    wait_pos(act, gu_done, t * 32 - 16)
                if mat == UP:
                    wait_pos(act, gu_done, t * 32)
                if mat == DOWN:
                    wait_pos(act, down_done, t * 16)
                bank = psum[:, 7 if mat == UP else 6, :].bitcast(F16)
                run(q_t[:, mat, :, :].rearrange("p k o -> p (k o)"), bank, ACT.Copy).then_inc(q_ready[mat], 1)

            def slot(half, base=0):
                return psum[:, base + 2 * half:base + 2 * half + 2, :].rearrange("p b c -> p (b c)")

            def first_group(t, mat, half):
                acc_of, scale = (g_acc, gate_scale) if mat == GATE else (u_acc, up_scale)
                act.wait_ge(gu_done, t * 32 + (16 * mat + half + 1))
                if mat == UP:
                    wait_pos(act, h_done, t * 2 + (half - 1))
                else:
                    wait_pos(act, silu_done, t * 2 + (half - 1))
                anchor(act)
                run(acc_of[:, half, :], slot(half), ACT.Copy,
                    scale=scale[:, :, :].rearrange("p t k -> p (t k)")[:, bass.ds(t * KT, 1)]).then_inc(gu_first, 1)

            def silu(t, half):
                act.wait_ge(gu_added, t * 28 + (12 + half + 1))
                wait_pos(act, h_lo, t * 2 + (half - 1))
                wait_pos(act, h_hi, t * 2 + (half - 1))
                run(h_sb[:, half, :], g_acc[:, half, :], ACT.Silu).then_inc(silu_done, 1)

            def hidden_hi(t, half):
                act.wait_ge(h_done, t * 2 + (half + 1))
                run(h_part(t, half, HI), h_sb[:, half, :], ACT.Copy).then_inc(h_hi, 1)

            def down_copy(t, d, at=None):
                n = t * 16 + (d + 1) if at is None else at + 1
                act.wait_ge(down_done, n)
                act.wait_ge(down_added, n)
                anchor(act)
                run(down_tmp[:, (d if at is None else at) % 2, :], slot(0, 4), ACT.Copy,
                    scale=down_scale[:, :, :].rearrange("p h t -> p (h t)")[:, bass.ds(t + (d % 8) * NI, 1)])\
                    .then_inc(down_copied, 1)

            def keep_last():
                act.wait_ge(q_turned[DOWN], NI)
                act.wait_ge(down_done, TAIL_FROM + len([1 for t, _ in TAIL_POOL if t == NI - 2]))
                act.wait_ge(tail_done, len([1 for t, _, by_pool in TAIL if t == NI - 2 and not by_pool]))
                run(q_t[:, DOWN, :, :].rearrange("p k o -> p (k o)"), psum[:, 6, :].bitcast(F16), ACT.Copy)\
                    .then_inc(q_ready[DOWN], 1)

            conv(GATE, 0)
            conv(UP, 0)
            keep(GATE, 0)
            keep(UP, 0)

            def tile(t):
                for idx in range(32):
                    if idx in (0, 1, 16, 17):
                        first_group(t, idx // 16, idx % 2)
                    for back, d in downs(t, idx):
                        down_copy(t - back, d)
                    if idx == 3 and has_prev(t):
                        keep(UP, t)
                    if idx == CONV_DOWN and has_prev(t):
                        conv(DOWN, t - 1)
                    if idx in (7, 9) and has_prev(t):
                        hidden_hi(t - 1, (idx - 7) // 2)
                    if idx == CONV_GATE and has_next(t):
                        conv(GATE, t + 1)
                    if idx == 17 and has_prev(t):
                        keep(DOWN, t - 1)
                    if idx in (20, 24):
                        silu(t, (idx - 20) // 4)
                    if idx == CONV_UP and has_next(t):
                        conv(UP, t + 1)
                    if idx == TURN_GATE + 3 and has_next(t):
                        keep(GATE, t + 1)

            tiles(act, tile)
            conv(DOWN, NI - 1)
            hidden_hi(NI - 1, 0)
            hidden_hi(NI - 1, 1)
            for n, (t, d) in enumerate(TAIL_POOL):
                if (t, d) == (NI - 1, 0):
                    keep_last()
                down_copy(t, d, TAIL_FROM + n)

        @block.vector
        def _(dve):
            v = nc.vector

            def pair_of(n):
                return pair(n).rearrange("p (k r) -> p k r", r=P)

            def layer_stats(i):
                dve.wait_ge(x_loaded, i * 16 + 16)
                for c in range(2):
                    v.bn_stats(stats[:, c, :], x_tile[:, c * 512:(c + 1) * 512]).then_inc(ln_stats, 1)
                dve.wait_ge(ln_stats, i * 2 + 2)
                anchor(dve)
                v.bn_aggr(ln_small[:, 0:2], stats[:, :, :]).then_inc(ln_mv, 1)
                dve.wait_ge(ln_mv, i + 1)
                v.tensor_scalar(ln_small[:, 2:3], ln_small[:, 1:2], EPS, None, ALU.add).then_inc(ln_var, 1)

            def layer_norm(i):
                dve.wait_ge(ln_std, i + 1)
                v.reciprocal(ln_small[:, 4:5], ln_small[:, 3:4]).then_inc(ln_rstd, 1)
                dve.wait_ge(ln_rstd, i + 1)
                v.tensor_scalar(x_tile[:], x_tile[:], ln_small[:, 0:1], ln_small[:, 4:5],
                                ALU.subtract, ALU.mult).then_inc(xn_ready, 1)

            def x_part(i):
                flat = xt_tile[:, :, :].rearrange("p a b -> p (a b)")
                dve.wait_ge(x_hi, i + 1)
                v.tensor_tensor(flat[:, bass.ds((i % 2) * (2 * KT * P) + KT * P, KT * P)], pair(0),
                                flat[:, bass.ds((i % 2) * (2 * KT * P), KT * P)], ALU.subtract).then_inc(x_lo, 1)

            def weights(w4):
                for w in range(4 * w4, 4 * w4 + 4):
                    at = slice((w % KT) * P, (w % KT + 1) * P)
                    dve.wait_ge(w_hi, w + 1)
                    v.scalar_tensor_tensor(out=wt[:, LO, w // KT, :, at], in0=pair_of(w % 2), scalar=W_SCALE,
                                           in1=wt[:, HI, w // KT, :, at], op0=ALU.mult,
                                           op1=ALU.subtract).then_inc(w_lo, 1)

            def unit_copy(i, u):
                dve.wait_ge(unit_done, i * 6 + (u + 1))
                wait_pos(dve, unit_lo, i * 6 + (u - 1))
                v.scalar_tensor_tensor(out=unit32[:, u % 2, :], in0=psum[:, u % 2, :], scalar=W_UNSCALE,
                                       in1=bias_qkv[:, u // 2, (u % 2) * BANK:(u % 2 + 1) * BANK],
                                       op0=ALU.mult, op1=ALU.add).then_inc(unit_copied, 1)

            def batch_copy(j, m):
                dve.wait_ge(batch_done, j * 16 + (m + 1))
                dst = batch_dest(dve, j, m)
                v.tensor_copy(dst, batch_source(m)).then_inc(batch_out[1], 1)

            def over_heads(ap):
                return ap.rearrange("p (g a) -> p g a", a=1).broadcast_to((P, GROUPS, DH))

            def softmax_shift(j):
                dve.wait_ge(s_out, j * 4 + 4)
                v.tensor_reduce(sums[:, 0, :], s_c[:], AX_X, ALU.max).then_inc(row_max, 1)
                dve.wait_ge(row_max, j + 1)
                wait_pos(dve, p_lo, j * 4)
                v.tensor_tensor(p_c[:], s_c[:], over_heads(sums[:, 0, :]), ALU.subtract).then_inc(shifted, 1)

            def softmax_mask(j):
                dve.wait_ge(exp_done, j + 1)
                v.scalar_tensor_tensor(out=p_c[:], in0=s_c[:], scalar=THRESH, in1=p_c[:],
                                       op0=ALU.is_gt, op1=ALU.mult).then_inc(mask_done, 1)
                dve.wait_ge(mask_done, j + 1)
                v.tensor_reduce(sums[:, 1, :], p_c[:], AX_X, ALU.add).then_inc(sum_done, 1)
                dve.wait_ge(sum_done, j + 1)
                v.reciprocal(sums[:, 2, :], sums[:, 1, :]).then_inc(recip_done, 1)
                dve.wait_ge(recip_done, j + 1)
                v.tensor_tensor(p_c[:], p_c[:], over_heads(sums[:, 2, :]), ALU.mult).then_inc(norm_done, 1)

            def head_copies(j, k):
                dve.wait_ge(pv_done, j * 4 + (k + 1))
                if k == 0:
                    wait_pos(dve, ctx_lo, j)
                block_copies(j, k, (2, 3), lambda d, s: v.tensor_copy(d, s), pv_out[1])

            def wo_part(n):
                dve.wait_ge(wo_hi, n + 1)
                v.scalar_tensor_tensor(out=wo_t[:, LO, :, n * P:(n + 1) * P],
                                       in0=psum[:, 0:2, :].rearrange("p b (k r) -> p (b k) r", r=P),
                                       scalar=W_SCALE, in1=wo_t[:, HI, :, n * P:(n + 1) * P], op0=ALU.mult,
                                       op1=ALU.subtract).then_inc(wo_lo, 1)

            def tile_2(i):
                more = not isinstance(i, int) or i + 1 < TT
                for s in range(QUARTERS):
                    if s % 4 == 3 and projects(i):
                        unit_copy(i, s // 4)
                    if not projects(i) and s < KT:
                        wo_part(s)
                    for kind, n in steps_of(i, s):
                        if kind == "X":
                            x_part(i + 1)
                        elif kind == "T" and n % 2:
                            batch_copy(i - 1, n)
                        elif kind == "V":
                            head_copies(i - 1, n)
                    if s == STATS_AT and more:
                        layer_stats(i + 1)
                    if s == NORM_AT and more:
                        layer_norm(i + 1)
                    if s == SHIFT_AT:
                        softmax_shift(i - 1)
                    if s == MASK_AT:
                        softmax_mask(i - 1)

            layer_stats(0)
            layer_norm(0)

            def first_unit(u):
                if u == 0:
                    dve.wait_ge(bias_loaded, 4 * 16)
                unit_copy(0, u)

            def next_x():
                layer_stats(1)
                layer_norm(1)
                x_part(1)

            walk(dve, lambda: opening(weights, lambda: x_part(0), first_unit, next_x), tile_2)

            dve.wait_ge(scales_loaded, 3 * 16)

            def add_group(t, idx):
                mat, g, half = idx // 16, idx // 2 % 8, idx % 2
                acc_of, scale = (g_acc, gate_scale) if mat == GATE else (u_acc, up_scale)
                before = 14 * mat + 2 * (g - 1) + half
                dve.wait_ge(gu_done, t * 32 + (idx + 1))
                if g == 1:
                    dve.wait_ge(gu_first, t * 4 + (2 * mat + half + 1))
                else:
                    dve.wait_ge(gu_added, t * 28 + (before - 2 + 1))
                v.scalar_tensor_tensor(
                    out=acc_of[:, half, :], in0=psum[:, 2 * half:2 * half + 2, :].rearrange("p b c -> p (b c)"),
                    scalar=scale[:, :, :].rearrange("p t k -> p (t k)")[:, bass.ds(t * KT + g, 1)],
                    in1=acc_of[:, half, :], op0=ALU.mult, op1=ALU.add).then_inc(gu_added, 1)

            def hidden(t, half):
                dve.wait_ge(silu_done, t * 2 + (half + 1))
                dve.wait_ge(gu_added, t * 28 + (26 + half + 1))
                v.tensor_tensor(h_sb[:, half, :], h_sb[:, half, :], u_acc[:, half, :], ALU.mult).then_inc(h_done, 1)

            def hidden_lo(t, half):
                dve.wait_ge(h_hi, t * 2 + (half + 1))
                v.tensor_tensor(h_part(t, half, LO), h_sb[:, half, :], h_part(t, half, HI), ALU.subtract)\
                    .then_inc(h_lo, 1)

            def tile(t):
                if has_prev(t):
                    hidden(t - 1, 0)
                    hidden(t - 1, 1)
                for idx in range(32):
                    if idx // 2 % 8:
                        add_group(t, idx)
                    if idx in (16, 17) and has_prev(t):
                        hidden_lo(t - 1, idx - 16)

            tiles(dve, tile)
            hidden(NI - 1, 0)
            hidden(NI - 1, 1)
            fast = 0
            dve.wait_ge(down_added, 2 + TAIL_FROM)
            for t, d, by_pool in TAIL:
                if fast in (0, 2) and not by_pool:
                    hidden_lo(NI - 1, fast // 2)
                if not by_pool:
                    half, ho = d // 8, d % 8
                    dve.wait_ge(tail_done, fast + 1)
                    wait_pos(dve, tail_added, fast)
                    v.scalar_tensor_tensor(
                        out=acc[:, half, ho, :], in0=psum[:, 2 * (fast % 2):2 * (fast % 2) + 2, :]
                        .rearrange("p b c -> p (b c)"), scalar=down_scale[:, ho, t:t + 1],
                        in1=acc[:, half, ho, :], op0=ALU.mult, op1=ALU.add).then_inc(tail_added, 1)
                    fast += 1

            def residual(u, n, x_count):
                dve.wait_ge(y_turned, u + 1)
                dve.wait_ge(res_loaded[n], x_count)
                v.tensor_tensor(x_res[:, n, :], psum[:, 2 * n:2 * n + 2, :].rearrange("p b c -> p (b c)"),
                                x_res[:, n, :], ALU.add).then_inc(y_ready, 1)

            with dve.Fori(0, TT // 4) as m:
                for n in range(4):
                    residual(m * 4 + n, n, m * 16 + 16)

        @block.gpsimd
        def _(pool):
            g = nc.gpsimd
            g.memset(ident32[:], 0.0).then_inc(const_mem, 1)
            g.memset(ident16[:], 0.0).then_inc(const_mem, 1)
            pool.wait_ge(const_mem, 2)
            for m in (ident32, ident16):
                g.affine_select(out=m[:], in_=m[:], compare_op=ALU.not_equal, fill=1.0, base=0,
                                pattern=[[-1, P]], channel_multiplier=1).then_inc(const_ready, 1)

            def lo_part(dst, src, hi):
                return g.tensor_tensor(dst, src, hi, ALU.subtract)

            def unit_part(i, u):
                pool.wait_ge(unit_hi, i * 6 + (u + 1))
                src, hi = unit_view(u), stack_view(u, HI)
                for n in range(2):
                    last = lo_part(stack_view(u, LO)[n], src, hi[n])
                last.then_inc(unit_lo, 1)

            def prob_lo(j, q):
                pool.wait_ge(p_hi, j * 4 + (q + 1))
                at = slice(8 * q, 8 * q + 8)
                for n in range(2):
                    last = lo_part(p_stack[:, at, 2 + n, :], p_c[:, at, :], p_stack[:, at, n, :])
                last.then_inc(p_lo, 1)

            def context_lo(j):
                pool.wait_ge(ctx_hi, j + 1)
                lo_part(ctx_parts[:, LO, :, :], ctx_32[:], ctx_parts[:, HI, :, :]).then_inc(ctx_lo, 1)

            def tile_2(i):
                for s in range(QUARTERS):
                    if s == P_AT:
                        for q in range(4):
                            prob_lo(i - 1, q)
                    if s % 4 == 3 and projects(i):
                        unit_part(i, s // 4)
                context_lo(i - 1)

            def first_units():
                for u in range(6):
                    unit_part(0, u)

            walk(pool, first_units, tile_2)

            pool.sem_inc(down_added, 2)

            def add_down(at, half, ho):
                pool.wait_ge(down_copied, at + 2)
                pool.wait_ge(down_added, at + 1)
                g.tensor_tensor(acc[:, half, ho, :], acc[:, half, ho, :], down_tmp[:, (half * 8 + ho) % 2
                                if not isinstance(at, int) else at % 2, :], ALU.add).then_inc(down_added, 1)

            with pool.Fori(0, NI - 2) as t:
                for d in range(16):
                    add_down(t * 16 + d, d // 8, d % 8)
            for d in range(EARLY):
                add_down(16 * (NI - 2) + d, 0, d)
            for n, (t, d) in enumerate(TAIL_POOL):
                add_down(TAIL_FROM + n, d // 8, d % 8)

        @block.sync
        def _(sp):
            sp.dma_start(x_tile[:], x_rows[0:P, :]).then_inc(x_loaded, 16)

            def load_w(w):
                if w >= 4:
                    sp.wait_ge(w_turned, w - 3)
                sp.dma_start(w_rows[:, w % 4, :], (Wq, Wk, Wv)[w // KT][(w % KT) * P:(w % KT + 1) * P, :])\
                    .then_inc(w_loaded[w % 4], 16)

            for w in range(8):
                load_w(w)
            for r, b in enumerate((bq, bk, bv)):
                sp.dma_start(bias_qkv[:, r, :], b.rearrange("(a n) -> a n", a=1).broadcast_to((P, H)))\
                    .then_inc(bias_loaded, 16)
            sp.dma_start(bias_o[:], bo.rearrange("(g p) -> p g", p=P),
                         allow_slow_non_contiguous=True).then_inc(bias_loaded, 16)
            for w in range(8, 3 * KT):
                load_w(w)

            def load_x(i):
                sp.wait_ge(x_turned, i)
                sp.dma_start(x_tile[:], x_rows[bass.ds(i * P, P), :]).then_inc(x_loaded, 16)

            def store_xt(i):
                sp.wait_ge(x_lo, i + 1)
                anchor(sp)
                src = xt_tile[:, :, :].rearrange("p a b -> p (a b)")[:, bass.ds((i % 2) * (2 * KT * P), 2 * KT * P)]
                sp.dma_start(xt_dram.rearrange("t p a k c -> t p (a k c)")[bass.ds(i, 1), :, :]
                             .rearrange("t p c -> (t p) c"), src).then_inc(xt_stored, 16)

            def store_context(j):
                sp.wait_ge(ctx_lo, j + 1)
                anchor(sp)
                sp.dma_start(ctx_dram.rearrange("t p a k c -> t p (a k c)")[bass.ds(j, 1), :, :]
                             .rearrange("t p c -> (t p) c"),
                             ctx_parts[:, :, :, :].rearrange("p a k c -> p (a k c)")).then_inc(ctx_stored, 16)

            def load_context(c):
                sp.dma_start(ctx_t[:, c % 2, :, :, :, :].rearrange("p t a k c -> p t (a k c)"),
                             ctx_dram[c * CT:(c + 1) * CT].rearrange("t p a k c -> p t (a k c)"))\
                    .then_inc(ctx_loaded[c % 2], 16)

            def load_wo(n):
                if n >= 2:
                    sp.wait_ge(wo_turned, n - 1)
                sp.dma_start(wo_rows[:, n % 2, :], Wo[n * P:(n + 1) * P, :]).then_inc(wo_loaded[n % 2], 16)

            def tile_2(i):
                if not isinstance(i, int) or i + 1 < TT:
                    load_x(i + 1)
                    store_xt(i + 1)
                if not projects(i):
                    sp.wait_ge(unit_done, 6 * TT)
                    sp.wait_ge(unit_copied, 6 * TT)
                    load_wo(0)
                    load_wo(1)
                    sp.wait_ge(ctx_stored, 16 * 2 * CT)
                    load_context(0)
                    for n in range(2, KT):
                        load_wo(n)
                    load_context(1)
                store_context(i - 1)

            def first():
                store_xt(0)
                load_x(1)
                store_xt(1)

            walk(sp, first, tile_2)

            sp.wait_ge(ctx_stored, 16 * TT)
            sp.wait_ge(xt_stored, 16 * TT)
            sp.wait_ge(pv_done, 4 * TT)
            for dst, s_in in ((gate_scale, gate_s), (up_scale, up_s)):
                sp.dma_start(dst[:], s_in.rearrange("(t p) g -> p t g", p=P)).then_inc(scales_loaded, 16)
            sp.dma_start(down_scale[:], down_s.rearrange("(h p) t -> p h t", p=P)).then_inc(scales_loaded, 16)
            for c in range(4):
                if c < 2:
                    sp.wait_ge(proj_done, KT * (c + 1))
                    load_context(c + 2)
                sp.dma_start(xt[:, c * CT:(c + 1) * CT, :, :, :].rearrange("p t a k c -> p t (a k c)"),
                             xt_dram[c * CT:(c + 1) * CT].rearrange("t p a k c -> p t (a k c)"))\
                    .then_inc(xt_loaded, 16)

            sp.wait_ge(proj_done, 4 * KT)

            def load_q(mat, t):
                wait_pos(sp, q_conv[mat], t)
                anchor(sp)
                if mat == DOWN:
                    sp.dma_start(q_raw[:, DOWN, :].rearrange("p (h i) -> p h i", i=P),
                                 down_q[:, bass.ds(t * P, P)].rearrange("(h p) i -> p h i", p=P))\
                        .then_inc(q_loaded[mat], 16)
                else:
                    src = gate_q if mat == GATE else up_q
                    sp.dma_start(q_raw[:, mat, :], src[bass.ds(t * P, P), :]).then_inc(q_loaded[mat], 16)

            for mat in (GATE, UP, DOWN):
                load_q(mat, 0)
            with sp.Fori(1, NI) as t:
                for mat in (GATE, UP, DOWN):
                    load_q(mat, t)

            for mat in (GATE, UP, DOWN):
                sp.wait_ge(q_turned[mat], NI)

            def load_res(u, n):
                sp.dma_start(x_res[:, n, :], x_rows[bass.ds(u * P, P), :]).then_inc(res_loaded[n], 16)

            for n in range(4):
                load_res(n, n)

            def store(u, n):
                sp.wait_ge(y_ready, u + 1)
                sp.dma_start(out_rows[bass.ds(u * P, P), :], x_res[:, n, :]).then_inc(y_stored[n], 16)

            with sp.Fori(1, TT // 4) as m:
                for n in range(4):
                    store(m * 4 + (n - 4), n)
                for n in range(4):
                    sp.wait_ge(y_stored[n], m * 16)
                    anchor(sp)
                    load_res(m * 4 + n, n)
            for n in range(4):
                store(TT - 4 + n, n)
            for n in range(4):
                sp.wait_ge(y_stored[n], 16 * TT // 4)


_INS = ["L0_attn_x", "L0_attn_Wq", "L0_attn_bq", "L0_attn_Wk", "L0_attn_bk", "L0_attn_Wv", "L0_attn_bv",
        "L0_attn_Wo", "L0_attn_bo", "L0_ffn_gate_q", "L0_ffn_gate_s", "L0_ffn_up_q", "L0_ffn_up_s",
        "L0_ffn_down_q", "L0_ffn_down_s"]
_OUTS = [((4, 512, 1024), "float32")]


def kernel(**inputs):
    import numpy as _np
    import concourse.bacc as _bacc
    from concourse import mybir as _mybir
    from concourse.bass_utils import run_bass_kernel_spmd as _run

    nc = _bacc.Bacc("TRN2", target_bir_lowering=False, num_devices=1)
    arrays, args = {}, []
    for name in _INS:
        a = _np.ascontiguousarray(inputs[name])
        arrays[f"in_{name}_dram"] = a
        args.append(nc.dram_tensor(f"in_{name}_dram", a.shape, _mybir.dt.from_np(a.dtype), kind="ExternalInput").ap())
    for i, (shape, dtype) in enumerate(_OUTS):
        dt = _mybir.dt.from_np(_np.dtype(dtype))
        args.append(nc.dram_tensor(f"out_{i}_dram", shape, dt, kind="ExternalOutput").ap())
    build(nc, *args)
    r = _run(nc, [arrays], core_ids=[0])
    got = tuple(r.results[0][f"out_{i}_dram"] for i in range(len(_OUTS)))
    return got[0]
```

```python
from contextlib import ExitStack

import numpy as np

import concourse.bass as bass
from concourse import mybir

F32 = mybir.dt.float32
F16 = mybir.dt.float16
I32 = mybir.dt.int32
ALU = mybir.AluOpType
ACT = mybir.ActivationFunctionType
AX_X = mybir.AxisListType.X

P = 128
HI, LO = 0, 1
BANK = 512


def build(nc, x_in, Wq, bq, Wk, bk, Wv, bv, Wo, bo, gate_q, gate_s, up_q, up_s, down_q, down_s, out):
    B, S, H = x_in.shape
    T = B * S
    KT = H // P
    DH = 32
    NH = H // DH
    TG = P // DH
    GROUPS = P // TG
    INTER = gate_q.shape[0]
    NI = INTER // P
    TT = T // P
    HALF = T // 2
    CHUNK = T // 4
    CT = CHUNK // P
    EPS = 1e-5
    THRESH = 0.001
    INV_SQRT_D = float(np.float32(1.0 / np.sqrt(DH)))
    W_SCALE = 64.0
    W_UNSCALE = 1.0 / W_SCALE
    assert CHUNK == BANK and KT == 8 and gate_s.shape[1] == KT and down_s.shape[1] == NI and NH == 32

    x_rows = x_in.rearrange("b s h -> (b s) h")
    out_rows = out.rearrange("b s h -> (b s) h")
    ctx_dram = nc.dram_tensor("ctx_scratch", [TT, P, 2, KT, P], F16).ap()
    xt_dram = nc.dram_tensor("xt_scratch", [TT, P, 2, KT, P], F16).ap()

    with ExitStack() as whole:
        def sem(name):
            return whole.enter_context(nc.semaphore(name))

        def sb(stack, name, shape, dt):
            return stack.enter_context(nc.sbuf_tensor(name, shape, dt))

        ident32 = sb(whole, "ident32", [P, P], F32)
        ident16 = sb(whole, "ident16", [P, P], F16)
        bias_o = sb(whole, "bias_o", [P, KT], F32)
        psum = whole.enter_context(nc.psum_tensor("banks", [P, 8, BANK], F32))

        with ExitStack() as st:
            wt = sb(st, "wt", [P, 3, 2, KT, H], F16)
            bias_qkv = sb(st, "bias_qkv", [P, 3, H], F32)
            x_tile = sb(st, "x_tile", [P, H], F32)
            xt_tile = sb(st, "xt_tile", [P, 2, 2 * KT * P], F16)
            unit32 = sb(st, "unit32", [P, 2, BANK], F32)
            stats = sb(st, "stats", [P, 2, 6], F32)
            ln_small = sb(st, "ln_small", [P, 8], F32)
            sums = sb(st, "sums", [P, 3, GROUPS], F32)
            with ExitStack() as s1:
                w_rows = sb(s1, "w_rows", [P, 4, H], F32)
            with ExitStack() as s2:
                turned = sb(s2, "turned", [P, 3, P * NH], F16)
                probs_t = sb(s2, "probs_t", [P, GROUPS * P], F16)
                stacks = sb(s2, "stacks", [P, 3, NH, 4 * DH], F16)
                s_c = sb(s2, "s_c", [P, GROUPS, DH], F32)
                p_c = sb(s2, "p_c", [P, GROUPS, DH], F32)
                p_stack = sb(s2, "p_stack", [P, GROUPS, 4, DH], F16)
                ctx_32 = sb(s2, "ctx_32", [P, KT, P], F32)
                ctx_parts = sb(s2, "ctx_parts", [P, 2, KT, P], F16)

        LOWER = 74 * 1024
        lower = sb(whole, "lower", [P, LOWER // 4], F32)
        acc = sb(whole, "acc", [P, 2, KT, HALF], F32)
        xt = sb(whole, "xt", [P, TT, 2, KT, P], F16)
        gate_scale = sb(whole, "gate_scale", [P, NI, KT], F32)
        up_scale = sb(whole, "up_scale", [P, NI, KT], F32)
        down_scale = sb(whole, "down_scale", [P, KT, NI], F32)

        def carve(*wanted):
            at, views = 0, []
            for shape, dt in wanted:
                n = int(np.prod(shape))
                words = n // 2 if dt == F16 else n
                view = lower[:, at:at + words]
                view = view if dt == F32 else view.bitcast(dt)
                names = "abcde"[:len(shape)]
                views.append(view.rearrange(f"p ({' '.join(names)}) -> p {' '.join(names)}",
                                            **dict(zip(names[1:], shape[1:]))))
                at += words
            assert at * 4 <= LOWER
            return views

        wo_rows, ctx_a, wo_t, ctx_b = carve(((2, H), F32), ((CT, 2, KT, P), F16), ((2, KT, H), F16),
                                            ((CT, 2, KT, P), F16))
        ctx_t = (ctx_a, ctx_b)
        q_raw, q_16, gu_t, down_t, g_acc, u_acc, h_sb, h_parts, down_tmp = carve(
            ((3, H), I32), ((3, H), F16), ((2, KT, P), F16), ((2, KT, P), F16), ((2, HALF), F32),
            ((2, HALF), F32), ((2, HALF), F32), ((2, 2, 2, HALF), F16), ((2, HALF), F32))
        x_res = xt[:, :, :, :, :].rearrange("p t a k c -> p (t a k c)").bitcast(F32)\
            .rearrange("p (t h) -> p t h", h=H)

        const_mem = sem("const_mem")
        const_ready = sem("const_ready")
        w_loaded = [sem(f"w_loaded{k}") for k in range(4)]
        w_turned = sem("w_turned")
        w_hi = sem("w_hi")
        w_lo = sem("w_lo")
        bias_loaded = sem("bias_loaded")
        x_loaded = sem("x_loaded")
        ln_stats = sem("ln_stats")
        ln_mv = sem("ln_mv")
        ln_var = sem("ln_var")
        ln_std = sem("ln_std")
        ln_rstd = sem("ln_rstd")
        xn_ready = sem("xn_ready")
        x_turned = sem("x_turned")
        x_hi = sem("x_hi")
        x_lo = sem("x_lo")
        xt_stored = sem("xt_stored")
        unit_done = sem("unit_done")
        unit_copied = sem("unit_copied")
        unit_hi = sem("unit_hi")
        unit_lo = sem("unit_lo")
        batch_done = sem("batch_done")
        batch_out = [sem("batch_out_act"), sem("batch_out_dve")]
        s_done = sem("s_done")
        s_out = sem("s_out")
        row_max = sem("row_max")
        shifted = sem("shifted")
        exp_done = sem("exp_done")
        mask_done = sem("mask_done")
        sum_done = sem("sum_done")
        recip_done = sem("recip_done")
        norm_done = sem("norm_done")
        p_hi = sem("p_hi")
        p_lo = sem("p_lo")
        pv_done = sem("pv_done")
        pv_out = [sem("pv_out_act"), sem("pv_out_dve")]
        ctx_hi = sem("ctx_hi")
        ctx_lo = sem("ctx_lo")
        ctx_stored = sem("ctx_stored")
        scales_loaded = sem("scales_loaded")
        xt_loaded = sem("xt_loaded")
        wo_loaded = [sem(f"wo_loaded{k}") for k in range(2)]
        wo_turned = sem("wo_turned")
        wo_hi = sem("wo_hi")
        wo_lo = sem("wo_lo")
        ctx_loaded = [sem(f"ctx_loaded{k}") for k in range(2)]
        proj_done = sem("proj_done")
        proj_out = sem("proj_out")
        q_loaded = [sem(f"q_loaded{k}") for k in range(3)]
        q_conv = [sem(f"q_conv{k}") for k in range(3)]
        q_turned = [sem(f"q_turned{k}") for k in range(3)]
        q_ready = [sem(f"q_ready{k}") for k in range(3)]
        gu_done = sem("gu_done")
        gu_first = sem("gu_first")
        gu_added = sem("gu_added")
        silu_done = sem("silu_done")
        h_done = sem("h_done")
        h_hi = sem("h_hi")
        h_lo = sem("h_lo")
        down_done = sem("down_done")
        down_copied = sem("down_copied")
        down_added = sem("down_added")
        tail_done = sem("tail_done")
        tail_added = sem("tail_added")
        res_loaded = [sem(f"res_loaded{k}") for k in range(4)]
        y_stored = sem("y_stored")

        anchors = sem("anchors")

        def anchor(eng):
            eng.sem_inc(anchors, 1)

        block = whole.enter_context(nc.Block())
        GATE, UP, DOWN = 0, 1, 2
        Q, K, V = 0, 1, 2

        STEPS = [["T0"], ["T1"], ["T2"], ["T3"], ["T4"], ["T5"], ["T6", "T7"], ["S0"], ["S1"], ["S2"],
                 ["S3"], ["T8"], ["T9"], ["T10"], ["T11"], ["X"], [], [], [], ["T12"], ["T13", "V0"],
                 ["T14", "V1"], ["T15", "V2"], ["V3"]]
        QUARTERS = len(STEPS)
        STATS_AT, ROOT_AT, NORM_AT, SHIFT_AT, EXP_AT, MASK_AT, DIVIDE_AT, P_AT = 6, 8, 9, 10, 11, 12, 13, 15
        CONTEXT_AT = 2
        LAST_UNITS = (QUARTERS - 2) // 2

        def walk(eng, first, body):
            first()
            body(1)
            with eng.Fori(2, TT - 1) as i:
                body(i)
            body(TT - 1)
            body(TT)

        NEXT_NORM = 18

        def opening(weights, first_x, quarter, next_norm, next_x):
            for w in range(4):
                weights(w)
            first_x()
            for w in range(4, 3 * KT):
                weights(w)
                quarter(w - 4)
                if w == NEXT_NORM:
                    next_norm()
            next_x()
            for s in range(3 * KT - 4, 3 * KT):
                quarter(s)

        def steps_of(i, s):
            for name in STEPS[s]:
                kind, n = name[0], int(name[1:] or 0)
                if kind == "X":
                    if not isinstance(i, int) or i + 1 < TT:
                        yield kind, n
                else:
                    yield kind, n

        def wo_half(part, n2):
            n, k = n2 // 2, 4 * (n2 % 2)
            return wo_t[:, part, k:k + 4, n * P:(n + 1) * P]

        def wo_bank():
            return psum[:, 1, :].rearrange("p (k r) -> p k r", r=P)

        def output_bank(n):
            return n % 2 if n > KT else 0

        def projects(i):
            return not (isinstance(i, int) and i == TT)

        def wait_pos(eng, s, value):
            if not isinstance(value, int) or value > 0:
                eng.wait_ge(s, value)

        BATCH_BANK = 2

        def pair(n):
            return psum[:, 4 + 2 * n:6 + 2 * n, :].rearrange("p b c -> p (b c)")

        X_TURN = 4

        def turn_of(w):
            return w if w < X_TURN else w + 1

        def weight_pair(w):
            n = (4, 6, 2)[turn_of(w) % 3]
            return psum[:, n:n + 2, :].rearrange("p b c -> p (b c)")

        def x_pair(i):
            return pair(1) if isinstance(i, int) and i < 2 else pair(0)

        def batch_bank(m):
            return psum[:, BATCH_BANK + m % 2, :].bitcast(F16)

        def s_pair(k):
            return k % 2

        def v_pair(k):
            return (k + 1) % 2

        def block_copies(j, k, rs, engine_copy, out_sem):
            src = pair(v_pair(k)).rearrange("p (g c) -> p g c", c=P)
            for r in rs:
                for h4 in range(TG):
                    s_ap = src[r * DH:(r + 1) * DH, :, r * DH:(r + 1) * DH]\
                        .rearrange("p g (a h) -> p h a g", h=TG)[:, h4, :, :]
                    d_ap = ctx_32[h4 * DH:(h4 + 1) * DH, :, :]\
                        .rearrange("p a (g r) -> p r a g", r=TG)[:, r, :, 8 * k:8 * k + 8]
                    last = engine_copy(d_ap, s_ap)
            last.then_inc(out_sem, 1)

        def unit_view(u):
            return unit32[:, u % 2, :].rearrange("p (h d) -> p h d", d=DH)

        def stack_view(u, part):
            mat, h0 = u // 2, (u % 2) * (NH // 2)
            places = ((0, 1) if part == HI else (2, 3)) if mat == 0 else ((0, 2) if part == HI else (1, 3))
            if mat < 2:
                return [stacks[:, mat, h0:h0 + NH // 2, n * DH:(n + 1) * DH] for n in places]
            by_dim = stacks[:, mat, :, :].rearrange("p d (n h) -> p n h d", h=DH)
            return [by_dim[:, n, h0:h0 + NH // 2, :] for n in places]

        def batch_dest(eng, j, m):
            if m < 8:
                wait_pos(eng, s_done, j * 4)
            else:
                wait_pos(eng, pv_done, j * 4)
            if m >= 12:
                return probs_t[:, (m - 12) * 8 * P:(m - 11) * 8 * P]
            return turned[:, m // 4, :].rearrange("p (t x) -> p t x", x=NH)[:, :, 8 * (m % 4):8 * (m % 4) + 8]

        def batch_source(m):
            return batch_bank(m) if m >= 12 else batch_bank(m).rearrange("p (x t) -> p t x", t=P)

        FIRST_DOWN = 20
        EARLY = 16 - FIRST_DOWN // 2

        def downs(t, idx):
            if idx % 2:
                return
            if idx >= FIRST_DOWN and has_prev(t):
                yield 1, (idx - FIRST_DOWN) // 2
            if idx < FIRST_DOWN and not (isinstance(t, int) and t < 2):
                yield 2, EARLY + idx // 2

        def downs_before(t, idx):
            if idx > FIRST_DOWN:
                return 16 * (t - 1) + (idx - FIRST_DOWN + 1) // 2
            if isinstance(t, int) and t < 2:
                return 0
            return 16 * (t - 2) + (EARLY + (idx + 1) // 2)

        def adds_to(idx):
            return idx - 2 * (1 + idx // 16)

        def has_prev(t):
            return not (isinstance(t, int) and t == 0)

        def has_next(t):
            return not (isinstance(t, int) and t == NI - 1)

        OUT = -1
        LEAD = 11
        TAIL = [(NI - 2, d) for d in range(EARLY, 16)] + [(NI - 1, d) for d in range(LEAD)]
        for d in range(LEAD, 16):
            TAIL += [(OUT, d - LEAD), (NI - 1, d)]
        TAIL += [(OUT, u) for u in range(16 - LEAD, TT)]

        def by_pool(item):
            return item[1] % 3 == (1 if item[0] == OUT else 0)

        TAIL_FROM = 16 * (NI - 2) + EARLY
        TAIL_POOL = [item for item in TAIL if by_pool(item)]
        TAIL_FAST = [item for item in TAIL if not by_pool(item)]

        def made_by(items, half):
            return 1 + max(n for n, (t, d) in enumerate(items) if t == NI - 1 and d // 8 == half)

        TURN_UP, TURN_DOWN, TURN_GATE = 5, 11, 25
        AFTER_TURN = {(TURN_UP + 1) // 2 + EARLY, (TURN_DOWN + 1) // 2 + EARLY, (TURN_GATE + 1 - FIRST_DOWN) // 2}

        def halves_of(d):
            return (1, 0) if d in AFTER_TURN else (0, 1)

        CONV_DOWN, CONV_GATE, CONV_UP = 7, 21, 27
        LAST_USE = (30, 31, 29)

        def gu_pair(n):
            return psum[:, 2 * n:2 * n + 2, :].rearrange("p b c -> p (b c)")

        def turned_weights(mat, t):
            if mat == DOWN:
                return down_t[:, :, :, :].rearrange("p a k o -> p (a k o)")[:, bass.ds((t % 2) * KT * P, KT * P)]
            return gu_t[:, mat, :, :].rearrange("p k o -> p (k o)")

        h_flat = h_parts.rearrange("p a b c d -> p (a b c d)")

        def h_part(t, half, part):
            return h_flat[:, bass.ds((t % 2) * (4 * HALF) + (half * 2 + part) * HALF, HALF)]

        def tiles(eng, body):
            body(0)
            body(1)
            with eng.Fori(2, NI - 1) as t:
                body(t)
            body(NI - 1)

        @block.tensor
        def _(pe):
            mm, turn = nc.tensor.matmul, nc.tensor.transpose
            pe.wait_ge(const_ready, 2)

            def weights(w):
                pe.wait_ge(w_loaded[w % 4], 16 * (w // 4 + 1))
                before = turn_of(w) - 3
                if before == X_TURN:
                    pe.wait_ge(x_hi, 1)
                    pe.wait_ge(x_lo, 1)
                elif before >= 0:
                    pe.wait_ge(w_hi, before + 1 if before < X_TURN else before)
                    pe.wait_ge(w_lo, before + 1 if before < X_TURN else before)
                for k in range(KT):
                    last = turn(weight_pair(w)[:, k * P:(k + 1) * P], w_rows[:, w % 4, k * P:(k + 1) * P],
                                ident32[:])
                last.then_inc(w_turned, 1)

            def turn_x(i):
                pe.wait_ge(xn_ready, i + 1)
                if isinstance(i, int) and i == 0:
                    pe.wait_ge(w_hi, X_TURN - 2)
                    pe.wait_ge(w_lo, X_TURN - 2)
                elif isinstance(i, int) and i == 1:
                    pe.wait_ge(w_hi, 3 * KT - 2)
                    pe.wait_ge(w_lo, 3 * KT - 2)
                else:
                    pe.wait_ge(s_out, (i - 2) * 4 + 3)
                for k in range(KT):
                    last = turn(x_pair(i)[:, k * P:(k + 1) * P], x_tile[:, k * P:(k + 1) * P], ident32[:])
                last.then_inc(x_turned, 1)

            def project(i, s):
                u, ks = s // 4, range(2 * (s % 4), 2 * (s % 4) + 2)
                if s == 0:
                    pe.wait_ge(x_lo, i + 1)
                    pe.wait_ge(x_hi, i + 1)
                if s % 4 == 0:
                    wait_pos(pe, unit_copied, i * 6 + (u - 1))
                for k in ks:
                    for n, (wp, xp) in enumerate(((HI, HI), (LO, HI), (HI, LO))):
                        at = (i % 2) * (2 * KT * P) + (xp * KT + k) * P
                        last = mm(psum[:, u % 2, :], xt_tile[:, :, :].rearrange("p a b -> p (a b)")[:, bass.ds(at, P)],
                                  wt[:, u // 2, wp, k, (u % 2) * BANK:(u % 2 + 1) * BANK],
                                  start=(k == 0 and n == 0), stop=(k == KT - 1 and n == 2))
                if s % 4 == 3:
                    last.then_inc(unit_done, 1)

            def batch(j, m):
                if m < 12 and m % 4 == 0:
                    pe.wait_ge(unit_lo, j * 6 + (2 * (m // 4) + 2))
                if m >= 12:
                    pe.wait_ge(p_lo, j * 4 + (m - 12 + 1))
                wait_pos(pe, batch_out[m % 2], j * 8 + m // 2)
                for n in range(8):
                    x = 8 * (m % 4) + n
                    src = stacks[:, m // 4, x, :] if m < 12 else p_stack[:, x, :, :].rearrange("p a b -> p (a b)")
                    last = turn(batch_bank(m)[:, n * P:(n + 1) * P], src, ident16[:])
                last.then_inc(batch_done, 1)

            def scores(j, k):
                if k == 0:
                    pe.wait_ge(batch_out[0], j * 8 + 4)
                    pe.wait_ge(batch_out[1], j * 8 + 4)
                    wait_pos(pe, pv_out[0], j * 4)
                    wait_pos(pe, pv_out[1], j * 4)
                elif k >= 2:
                    pe.wait_ge(s_out, j * 4 + (k - 1))
                for n in range(8):
                    at = (8 * k + n) * P
                    last = mm(pair(s_pair(k))[:, n * P:(n + 1) * P], turned[:, Q, at:at + P],
                              turned[:, K, at:at + P], start=True, stop=True)
                last.then_inc(s_done, 1)

            def head_products(j, k):
                if k == 0:
                    pe.wait_ge(batch_out[0], j * 8 + 6)
                    pe.wait_ge(batch_out[1], j * 8 + 6)
                    pe.wait_ge(s_out, j * 4 + 4)
                elif k == 1:
                    if not isinstance(j, int):
                        pe.wait_ge(x_lo, j + 3)
                        pe.wait_ge(x_hi, j + 3)
                    else:
                        pe.wait_ge(x_lo, min(j + 3, TT))
                        pe.wait_ge(x_hi, min(j + 3, TT))
                else:
                    pe.wait_ge(pv_out[0], j * 4 + (k - 1))
                    pe.wait_ge(pv_out[1], j * 4 + (k - 1))
                pe.wait_ge(batch_out[k % 2], j * 8 + (6 + k // 2 + 1))
                for n in range(8):
                    at = (8 * k + n) * P
                    last = mm(pair(v_pair(k))[:, n * P:(n + 1) * P], turned[:, V, at:at + P],
                              probs_t[:, at:at + P], start=True, stop=True)
                last.then_inc(pv_done, 1)

            def first_quarter(s):
                pe.wait_ge(w_hi, 4 * (s // 4) + 4)
                pe.wait_ge(w_lo, 4 * (s // 4) + 4)
                project(0, s)

            def turn_wo(n2):
                n, half = n2 // 2, n2 % 2
                pe.wait_ge(wo_loaded[n % 2], 16 * (n // 2 + 1))
                if n2 == 0:
                    pe.wait_ge(unit_copied, TT * 6)
                else:
                    pe.wait_ge(wo_hi, n2)
                    pe.wait_ge(wo_lo, n2)
                for k in range(4):
                    last = turn(psum[:, 1, k * P:(k + 1) * P],
                                wo_rows[:, n % 2, (4 * half + k) * P:(4 * half + k + 1) * P], ident32[:])
                last.then_inc(wo_turned, 1)

            def output_unit(n, ks):
                c, ho = n // KT, n % KT
                if ks[0] == 0:
                    if n < KT:
                        pe.wait_ge(wo_hi, 2 * n + 2)
                        pe.wait_ge(wo_lo, 2 * n + 2)
                    if ho == 0:
                        pe.wait_ge(ctx_loaded[c % 2], 16 * (c // 2 + 1))
                    if n and n != KT + 1:
                        pe.wait_ge(proj_out, n if n <= KT else n - 1)
                for k in ks:
                    for m, (wp, cp) in enumerate(((HI, HI), (HI, LO), (LO, HI))):
                        last = mm(psum[:, output_bank(n), :], wo_t[:, wp, k, ho * P:(ho + 1) * P],
                                  ctx_t[c % 2][:, :, cp, k, :], start=(k == 0 and m == 0),
                                  stop=(k == KT - 1 and m == 2))
                if ks[-1] == KT - 1:
                    last.then_inc(proj_done, 1)

            def tile_2(i):
                for s in range(QUARTERS):
                    if projects(i):
                        project(i, s)
                    else:
                        if s < 2 * KT:
                            turn_wo(s)
                        if s >= 2:
                            output_unit(s // 2 - 1, range(4 * (s % 2), 4 * (s % 2) + 4))
                    for kind, n in steps_of(i, s):
                        if kind == "X":
                            turn_x(i + 1)
                        elif kind == "T":
                            batch(i - 1, n)
                        elif kind == "S":
                            scores(i - 1, n)
                        else:
                            head_products(i - 1, n)

            walk(pe, lambda: opening(weights, lambda: turn_x(0), first_quarter, lambda: None,
                             lambda: turn_x(1)), tile_2)

            def turn_q(mat, t, downs_made):
                pe.wait_ge(q_conv[mat], t + 1)
                wait_pos(pe, down_copied, 2 * downs_made - 1)
                bank = psum[:, 6, :].bitcast(F16)
                for k in range(KT):
                    last = turn(bank[:, k * P:(k + 1) * P], q_16[:, mat, k * P:(k + 1) * P], ident16[:])
                last.then_inc(q_turned[mat], 1)

            for n in range(LAST_UNITS, 4 * KT):
                if n == 4 * KT - 1:
                    pe.wait_ge(pv_out[0], TT * 4)
                    pe.wait_ge(pv_out[1], TT * 4)
                    turn_q(GATE, 0, 0)
                    pe.wait_ge(q_ready[GATE], 1)
                    turn_q(UP, 0, 0)
                output_unit(n, range(KT))

            def gate_up(t, idx):
                mat, g, half = idx // 16, idx // 2 % 8, idx % 2
                if idx in (0, 16):
                    pe.wait_ge(q_ready[mat], t + 1)
                if idx >= 3 or has_prev(t):
                    tile_of, before = (t, idx - 3) if idx >= 3 else (t - 1, LAST_USE[idx])
                    if before // 2 % 8:
                        pe.wait_ge(gu_added, tile_of * 28 + (adds_to(before) + 1))
                    else:
                        pe.wait_ge(gu_first, tile_of * 4 + (2 * (before // 16) + before % 2 + 1))
                for c in range(2):
                    for part in (HI, LO):
                        last = mm(psum[:, 2 * (idx % 3) + c, :], gu_t[:, mat, g, :],
                                  xt[:, (2 * half + c) * CT:(2 * half + c + 1) * CT, part, g, :],
                                  start=(part == HI), stop=(part == LO))
                last.then_inc(gu_done, 1)

            def down_operands(t, d):
                if d == 0:
                    pe.wait_ge(q_ready[DOWN], t + 1)
                if d % 8 == 0:
                    pe.wait_ge(h_lo, t * 2 + (d // 8 + 1))

            def down_half(bank, t, d, c):
                half, ho = d // 8, d % 8
                weights = down_t[:, :, :, :].rearrange("p a k o -> p (a k o)")
                for part in (HI, LO):
                    at = (t % 2) * (4 * HALF) + ((half * 2 + part) * HALF + c * BANK)
                    last = mm(psum[:, bank, :], weights[:, bass.ds((t % 2) * (KT * P) + ho * P, P)],
                              h_flat[:, bass.ds(at, BANK)], start=(part == HI), stop=(part == LO))
                return last

            def down(t, d, n, order, order_before, turned=None):
                down_operands(t, d)
                for c in order:
                    wait_pos(pe, down_copied, 2 * n + (order_before.index(c) - 1))
                    if c == 0 and turned:
                        pe.wait_ge(q_ready[turned[0]], turned[1])
                    down_half(6 + c, t, d, c).then_inc(down_done, 1)

            pe.wait_ge(proj_out, 4 * KT)
            pe.wait_ge(xt_loaded, 4 * 16)

            def tile(t):
                for idx in range(32):
                    gate_up(t, idx)
                    for back, d in downs(t, idx):
                        turned = {TURN_UP + 1: (UP, t + 1), TURN_DOWN + 1: (DOWN, t)}.get(idx)
                        if idx == TURN_GATE + 1 and has_next(t):
                            turned = (GATE, t + 2)
                        down(t - back, d, 16 * (t - back) + d, halves_of(d), halves_of((d - 1) % 16), turned)
                    if idx == TURN_UP and has_prev(t):
                        turn_q(UP, t, downs_before(t, idx))
                    if idx == TURN_DOWN and has_prev(t):
                        if isinstance(t, int) and t == 1:
                            pe.wait_ge(q_ready[UP], t + 1)
                        turn_q(DOWN, t - 1, downs_before(t, idx))
                    if idx == TURN_GATE and has_next(t):
                        turn_q(GATE, t + 1, downs_before(t, idx))

            tiles(pe, tile)
            turn_q(DOWN, NI - 1, TAIL_FROM)
            pe.wait_ge(q_ready[DOWN], NI)
            fast = slow = 0
            def turn_out(u, pair_at, done, halves):
                for k in range(KT):
                    last = turn(psum[:, pair_at + k // 4, (k % 4) * P:(k % 4 + 1) * P],
                                acc[:, u // 8, k, (u % 8) * P:(u % 8 + 1) * P], ident32[:])
                    if k == KT - 1 or (halves and k == KT // 2 - 1):
                        last.then_inc(done, 1)

            for t, d in TAIL:
                pool_n = TAIL_FROM + slow
                if t == OUT and d % 8 == 0:
                    pe.wait_ge(down_added, 2 + TAIL_FROM + made_by(TAIL_POOL, d // 8))
                    pe.wait_ge(tail_added, made_by(TAIL_FAST, d // 8))
                if by_pool((t, d)):
                    if t == OUT:
                        pe.wait_ge(down_copied, 2 * pool_n)
                        turn_out(d, 6, down_done, True)
                    else:
                        down(t, d, pool_n, (0, 1), (0, 1))
                    slow += 1
                else:
                    if fast < 3:
                        pe.wait_ge(gu_added, (NI - 1) * 28 + adds_to(LAST_USE[fast]) + 1)
                    else:
                        pe.wait_ge(tail_added, fast - 2)
                    if t == OUT:
                        turn_out(d, 2 * (fast % 3), tail_done, False)
                    else:
                        down_operands(t, d)
                        down_half(2 * (fast % 3), t, d, 0)
                        down_half(2 * (fast % 3) + 1, t, d, 1).then_inc(tail_done, 1)
                    fast += 1

        @block.scalar
        def _(act):
            run = nc.scalar.activation

            def weights(w):
                act.wait_ge(w_turned, w + 1)
                run(wt[:, w // KT, HI, :, (w % KT) * P:(w % KT + 1) * P],
                    weight_pair(w).rearrange("p (k r) -> p k r", r=P), ACT.Copy,
                    scale=W_SCALE).then_inc(w_hi, 1)

            def root(i):
                act.wait_ge(ln_var, i + 1)
                run(ln_small[:, 3:4], ln_small[:, 2:3], ACT.Sqrt).then_inc(ln_std, 1)

            def x_part(i):
                act.wait_ge(x_turned, i + 1)
                wait_pos(act, xt_stored, i * 16 - 16)
                wait_pos(act, unit_done, i * 6 - 6)
                flat = xt_tile[:, :, :].rearrange("p a b -> p (a b)")
                run(flat[:, bass.ds((i % 2) * (2 * KT * P), KT * P)], x_pair(i), ACT.Copy).then_inc(x_hi, 1)

            def unit_part(i, u):
                act.wait_ge(unit_copied, i * 6 + (u + 1))
                if not isinstance(i, int) or i:
                    act.wait_ge(batch_done, i * 16 + (4 * (u // 2) - 12))
                dst, src = stack_view(u, HI), unit_view(u)
                for n in range(2):
                    last = run(dst[n], src, ACT.Copy)
                last.then_inc(unit_hi, 1)

            def batch_copy(j, m):
                act.wait_ge(batch_done, j * 16 + (m + 1))
                dst = batch_dest(act, j, m)
                run(dst, batch_source(m), ACT.Copy).then_inc(batch_out[0], 1)

            def scores_out(j, k):
                act.wait_ge(s_done, j * 4 + (k + 1))
                if k == 0:
                    wait_pos(act, mask_done, j)
                src = pair(s_pair(k)).rearrange("p (g c) -> p g c", c=P)
                for r in range(TG):
                    last = run(s_c[r * DH:(r + 1) * DH, 8 * k:8 * k + 8, :],
                               src[r * DH:(r + 1) * DH, :, r * DH:(r + 1) * DH], ACT.Copy, scale=INV_SQRT_D)
                last.then_inc(s_out, 1)

            def exponentials(j):
                act.wait_ge(shifted, j + 1)
                run(p_c[:], p_c[:], ACT.Exp).then_inc(exp_done, 1)

            def prob_hi(j, q):
                if q == 0:
                    act.wait_ge(norm_done, j + 1)
                wait_pos(act, batch_done, j * 16 + (q - 3))
                for n in range(2):
                    last = run(p_stack[:, 8 * q:8 * q + 8, n, :], p_c[:, 8 * q:8 * q + 8, :], ACT.Copy)
                last.then_inc(p_hi, 1)

            def context_hi(j):
                act.wait_ge(pv_out[0], j * 4 + 4)
                act.wait_ge(pv_out[1], j * 4 + 4)
                wait_pos(act, ctx_stored, j * 16)
                run(ctx_parts[:, HI, :, :], ctx_32[:], ACT.Copy).then_inc(ctx_hi, 1)

            def head_copies(j, k):
                act.wait_ge(pv_done, j * 4 + (k + 1))
                if k == 0:
                    wait_pos(act, ctx_lo, j)
                block_copies(j, k, (0, 1), lambda d, s: run(d, s, ACT.Copy), pv_out[0])

            def wo_part(n2):
                act.wait_ge(wo_turned, n2 + 1)
                if n2 == 0:
                    act.wait_ge(unit_done, 6 * TT)
                run(wo_half(HI, n2), wo_bank(), ACT.Copy, scale=W_SCALE).then_inc(wo_hi, 1)

            def output_out(n):
                c, ho = n // KT, n % KT
                act.wait_ge(proj_done, n + 1)
                run(acc[:, c // 2, ho, (c % 2) * CHUNK:(c % 2 + 1) * CHUNK], psum[:, output_bank(n), :], ACT.Identity,
                    bias=bias_o[:, ho:ho + 1], scale=W_UNSCALE).then_inc(proj_out, 1)

            def tile_2(i):
                for s in range(QUARTERS):
                    if s == CONTEXT_AT and not (isinstance(i, int) and i == 1):
                        context_hi(i - 2)
                    if not projects(i):
                        if s < 2 * KT:
                            wo_part(s)
                        if s > 2 and s % 2:
                            output_out(s // 2 - 1)
                    for kind, n in steps_of(i, s):
                        if kind == "X":
                            x_part(i + 1)
                        elif kind == "T" and n % 2 == 0:
                            batch_copy(i - 1, n)
                        elif kind == "S":
                            scores_out(i - 1, n)
                        elif kind == "V":
                            head_copies(i - 1, n)
                    if s == ROOT_AT and (not isinstance(i, int) or i + 1 < TT):
                        root(i + 1)
                    if s == EXP_AT:
                        exponentials(i - 1)
                    if s == P_AT:
                        for q in range(4):
                            prob_hi(i - 1, q)
                    if s % 4 == 3 and projects(i):
                        unit_part(i, s // 4)
                if not projects(i):
                    context_hi(i - 1)

            root(0)

            def first_quarter(s):
                if s % 4 == 0 and s:
                    unit_part(0, s // 4 - 1)
                if s == QUARTERS - 1:
                    unit_part(0, 5)

            walk(act, lambda: opening(weights, lambda: x_part(0), first_quarter, lambda: root(1),
                              lambda: x_part(1)), tile_2)

            def conv(mat, t):
                act.wait_ge(q_loaded[mat], t * 16 + 16)
                wait_pos(act, q_turned[mat], t)
                run(q_16[:, mat, :], q_raw[:, mat, :], ACT.Copy).then_inc(q_conv[mat], 1)

            def keep(mat, t):
                act.wait_ge(q_turned[mat], t + 1)
                if mat == GATE:
                    wait_pos(act, gu_done, t * 32 - 16)
                if mat == UP:
                    wait_pos(act, gu_done, t * 32)
                if mat == DOWN:
                    wait_pos(act, down_done, t * 32 - 32)
                run(turned_weights(mat, t), psum[:, 6, :].bitcast(F16), ACT.Copy)\
                    .then_inc(q_ready[mat], 1)

            act.wait_ge(xt_stored, 16 * TT)
            act.wait_ge(ctx_lo, TT)
            for n in range(LAST_UNITS, 4 * KT):
                if n == 4 * KT - 4:
                    conv(GATE, 0)
                    conv(UP, 0)
                if n == 4 * KT - 1:
                    keep(GATE, 0)
                    keep(UP, 0)
                output_out(n)

            act.wait_ge(scales_loaded, 3 * 16)

            def first_group(t, mat, half):
                acc_of, scale = (g_acc, gate_scale) if mat == GATE else (u_acc, up_scale)
                act.wait_ge(gu_done, t * 32 + (16 * mat + half + 1))
                if mat == UP:
                    wait_pos(act, h_done, t * 2 + (half - 1))
                else:
                    wait_pos(act, silu_done, t * 2 + (half - 1))
                anchor(act)
                run(acc_of[:, half, :], gu_pair((16 * mat + half) % 3), ACT.Copy,
                    scale=scale[:, :, :].rearrange("p t k -> p (t k)")[:, bass.ds(t * KT, 1)]).then_inc(gu_first, 1)

            def silu(t, half):
                act.wait_ge(gu_added, t * 28 + (12 + half + 1))
                wait_pos(act, h_lo, t * 2 + (half - 1))
                wait_pos(act, h_hi, t * 2 + (half - 1))
                run(h_sb[:, half, :], g_acc[:, half, :], ACT.Silu).then_inc(silu_done, 1)

            def hidden_hi(t, half):
                act.wait_ge(h_done, t * 2 + (half + 1))
                run(h_part(t, half, HI), h_sb[:, half, :], ACT.Copy).then_inc(h_hi, 1)

            def down_copy(t, d, n, order):
                scale = 1.0
                if not (isinstance(t, int) and t == OUT):
                    scale = down_scale[:, :, :].rearrange("p h t -> p (h t)")[:, bass.ds(t + (d % 8) * NI, 1)]
                act.wait_ge(down_added, n + 1)
                buffer = (n if isinstance(n, int) else d) % 2
                for m, c in enumerate(order):
                    act.wait_ge(down_done, 2 * n + (m + 1))
                    anchor(act)
                    run(down_tmp[:, buffer, c * BANK:(c + 1) * BANK], psum[:, 6 + c, :], ACT.Copy, scale=scale)\
                        .then_inc(down_copied, 1)

            def tile(t):
                for idx in range(32):
                    if idx in (0, 1, 16, 17):
                        first_group(t, idx // 16, idx % 2)
                    for back, d in downs(t, idx):
                        down_copy(t - back, d, 16 * (t - back) + d, halves_of(d))
                    if idx == TURN_UP and has_prev(t):
                        keep(UP, t)
                    if idx == CONV_DOWN and has_prev(t):
                        conv(DOWN, t - 1)
                    if idx == TURN_DOWN and has_prev(t):
                        keep(DOWN, t - 1)
                    if idx in (9, 13) and has_prev(t):
                        hidden_hi(t - 1, (idx - 9) // 4)
                    if idx in (19, 23):
                        silu(t, (idx - 19) // 4)
                    if idx == CONV_GATE and has_next(t):
                        conv(GATE, t + 1)
                    if idx == TURN_GATE and has_next(t):
                        keep(GATE, t + 1)
                    if idx == CONV_UP and has_next(t):
                        conv(UP, t + 1)

            tiles(act, tile)
            conv(DOWN, NI - 1)
            keep(DOWN, NI - 1)
            hidden_hi(NI - 1, 0)
            hidden_hi(NI - 1, 1)
            for n, (t, d) in enumerate(TAIL_POOL):
                down_copy(t, d, TAIL_FROM + n, (0, 1))

        @block.vector
        def _(dve):
            v = nc.vector

            def layer_stats(i):
                dve.wait_ge(x_loaded, i * 16 + 16)
                for c in range(2):
                    v.bn_stats(stats[:, c, :], x_tile[:, c * 512:(c + 1) * 512]).then_inc(ln_stats, 1)
                dve.wait_ge(ln_stats, i * 2 + 2)
                anchor(dve)
                v.bn_aggr(ln_small[:, 0:2], stats[:, :, :]).then_inc(ln_mv, 1)
                dve.wait_ge(ln_mv, i + 1)
                v.tensor_scalar(ln_small[:, 2:3], ln_small[:, 1:2], EPS, None, ALU.add).then_inc(ln_var, 1)

            def layer_norm(i):
                dve.wait_ge(ln_std, i + 1)
                v.reciprocal(ln_small[:, 4:5], ln_small[:, 3:4]).then_inc(ln_rstd, 1)
                dve.wait_ge(ln_rstd, i + 1)
                v.tensor_scalar(x_tile[:], x_tile[:], ln_small[:, 0:1], ln_small[:, 4:5],
                                ALU.subtract, ALU.mult).then_inc(xn_ready, 1)

            def x_part(i):
                flat = xt_tile[:, :, :].rearrange("p a b -> p (a b)")
                dve.wait_ge(x_hi, i + 1)
                v.tensor_tensor(flat[:, bass.ds((i % 2) * (2 * KT * P) + KT * P, KT * P)], x_pair(i),
                                flat[:, bass.ds((i % 2) * (2 * KT * P), KT * P)], ALU.subtract).then_inc(x_lo, 1)

            def weights(w):
                at = slice((w % KT) * P, (w % KT + 1) * P)
                dve.wait_ge(w_hi, w + 1)
                v.scalar_tensor_tensor(out=wt[:, w // KT, LO, :, at],
                                       in0=weight_pair(w).rearrange("p (k r) -> p k r", r=P), scalar=W_SCALE,
                                       in1=wt[:, w // KT, HI, :, at], op0=ALU.mult,
                                       op1=ALU.subtract).then_inc(w_lo, 1)

            def unit_copy(i, u):
                dve.wait_ge(unit_done, i * 6 + (u + 1))
                wait_pos(dve, unit_lo, i * 6 + (u - 1))
                v.scalar_tensor_tensor(out=unit32[:, u % 2, :], in0=psum[:, u % 2, :], scalar=W_UNSCALE,
                                       in1=bias_qkv[:, u // 2, (u % 2) * BANK:(u % 2 + 1) * BANK],
                                       op0=ALU.mult, op1=ALU.add).then_inc(unit_copied, 1)

            def batch_copy(j, m):
                dve.wait_ge(batch_done, j * 16 + (m + 1))
                dst = batch_dest(dve, j, m)
                v.tensor_copy(dst, batch_source(m)).then_inc(batch_out[1], 1)

            def over_heads(ap):
                return ap.rearrange("p (g a) -> p g a", a=1).broadcast_to((P, GROUPS, DH))

            def softmax_shift(j):
                dve.wait_ge(s_out, j * 4 + 4)
                v.tensor_reduce(sums[:, 0, :], s_c[:], AX_X, ALU.max).then_inc(row_max, 1)
                dve.wait_ge(row_max, j + 1)
                wait_pos(dve, p_lo, j * 4)
                v.tensor_tensor(p_c[:], s_c[:], over_heads(sums[:, 0, :]), ALU.subtract).then_inc(shifted, 1)

            def softmax_mask(j):
                dve.wait_ge(exp_done, j + 1)
                v.scalar_tensor_tensor(out=p_c[:], in0=s_c[:], scalar=THRESH, in1=p_c[:],
                                       op0=ALU.is_gt, op1=ALU.mult).then_inc(mask_done, 1)
                dve.wait_ge(mask_done, j + 1)
                v.tensor_reduce(sums[:, 1, :], p_c[:], AX_X, ALU.add).then_inc(sum_done, 1)

            def softmax_divide(j):
                dve.wait_ge(sum_done, j + 1)
                v.reciprocal(sums[:, 2, :], sums[:, 1, :]).then_inc(recip_done, 1)
                dve.wait_ge(recip_done, j + 1)
                v.tensor_tensor(p_c[:], p_c[:], over_heads(sums[:, 2, :]), ALU.mult).then_inc(norm_done, 1)

            def head_copies(j, k):
                dve.wait_ge(pv_done, j * 4 + (k + 1))
                if k == 0:
                    wait_pos(dve, ctx_lo, j)
                block_copies(j, k, (2, 3), lambda d, s: v.tensor_copy(d, s), pv_out[1])

            def wo_part(n2):
                dve.wait_ge(wo_hi, n2 + 1)
                v.scalar_tensor_tensor(out=wo_half(LO, n2), in0=wo_bank(), scalar=W_SCALE, in1=wo_half(HI, n2),
                                       op0=ALU.mult, op1=ALU.subtract).then_inc(wo_lo, 1)

            def tile_2(i):
                more = not isinstance(i, int) or i + 1 < TT
                for s in range(QUARTERS):
                    if s % 4 == 3 and projects(i):
                        unit_copy(i, s // 4)
                    if not projects(i) and s < 2 * KT:
                        wo_part(s)
                    for kind, n in steps_of(i, s):
                        if kind == "X":
                            x_part(i + 1)
                        elif kind == "T" and n % 2:
                            batch_copy(i - 1, n)
                        elif kind == "V":
                            head_copies(i - 1, n)
                    if s == STATS_AT and more:
                        layer_stats(i + 1)
                    if s == NORM_AT and more:
                        layer_norm(i + 1)
                    if s == SHIFT_AT:
                        softmax_shift(i - 1)
                    if s == MASK_AT:
                        softmax_mask(i - 1)
                    if s == DIVIDE_AT:
                        softmax_divide(i - 1)

            layer_stats(0)
            layer_norm(0)

            def first_quarter(s):
                if s == 4:
                    dve.wait_ge(bias_loaded, 4 * 16)
                if s % 4 == 0 and s:
                    unit_copy(0, s // 4 - 1)
                if s == QUARTERS - 1:
                    unit_copy(0, 5)

            def next_norm():
                layer_stats(1)
                layer_norm(1)

            walk(dve, lambda: opening(weights, lambda: x_part(0), first_quarter, next_norm,
                              lambda: x_part(1)), tile_2)

            dve.wait_ge(scales_loaded, 3 * 16)

            def add_group(t, idx):
                mat, g, half = idx // 16, idx // 2 % 8, idx % 2
                acc_of, scale = (g_acc, gate_scale) if mat == GATE else (u_acc, up_scale)
                before = 14 * mat + 2 * (g - 1) + half
                dve.wait_ge(gu_done, t * 32 + (idx + 1))
                if g == 1:
                    dve.wait_ge(gu_first, t * 4 + (2 * mat + half + 1))
                else:
                    dve.wait_ge(gu_added, t * 28 + (before - 2 + 1))
                v.scalar_tensor_tensor(
                    out=acc_of[:, half, :], in0=gu_pair(idx % 3),
                    scalar=scale[:, :, :].rearrange("p t k -> p (t k)")[:, bass.ds(t * KT + g, 1)],
                    in1=acc_of[:, half, :], op0=ALU.mult, op1=ALU.add).then_inc(gu_added, 1)

            def hidden(t, half):
                dve.wait_ge(silu_done, t * 2 + (half + 1))
                dve.wait_ge(gu_added, t * 28 + (26 + half + 1))
                v.tensor_tensor(h_sb[:, half, :], h_sb[:, half, :], u_acc[:, half, :], ALU.mult).then_inc(h_done, 1)

            def hidden_lo(t, half):
                dve.wait_ge(h_hi, t * 2 + (half + 1))
                v.tensor_tensor(h_part(t, half, LO), h_sb[:, half, :], h_part(t, half, HI), ALU.subtract)\
                    .then_inc(h_lo, 1)

            def tile(t):
                if has_prev(t):
                    hidden(t - 1, 0)
                    hidden(t - 1, 1)
                for idx in range(32):
                    if idx // 2 % 8:
                        add_group(t, idx)
                    if idx in (16, 17) and has_prev(t):
                        hidden_lo(t - 1, idx - 16)

            tiles(dve, tile)
            hidden(NI - 1, 0)
            hidden(NI - 1, 1)
            dve.wait_ge(down_added, 2 + TAIL_FROM)
            for n, (t, d) in enumerate(TAIL_FAST):
                if n in (0, 2):
                    hidden_lo(NI - 1, n // 2)
                dve.wait_ge(tail_done, n + 1)
                if t == OUT:
                    dve.wait_ge(res_loaded[d // 4], 16)
                    v.tensor_tensor(x_res[:, d, :], gu_pair(n % 3), x_res[:, d, :], ALU.add).then_inc(tail_added, 1)
                else:
                    half, ho = d // 8, d % 8
                    if (t - 1, d) in TAIL_FAST:
                        dve.wait_ge(tail_added, TAIL_FAST.index((t - 1, d)) + 1)
                    v.scalar_tensor_tensor(
                        out=acc[:, half, ho, :], in0=gu_pair(n % 3), scalar=down_scale[:, ho, t:t + 1],
                        in1=acc[:, half, ho, :], op0=ALU.mult, op1=ALU.add).then_inc(tail_added, 1)

        @block.gpsimd
        def _(pool):
            g = nc.gpsimd
            g.memset(ident32[:], 0.0).then_inc(const_mem, 1)
            g.memset(ident16[:], 0.0).then_inc(const_mem, 1)
            pool.wait_ge(const_mem, 2)
            for m in (ident32, ident16):
                g.affine_select(out=m[:], in_=m[:], compare_op=ALU.not_equal, fill=1.0, base=0,
                                pattern=[[-1, P]], channel_multiplier=1).then_inc(const_ready, 1)

            def lo_part(dst, src, hi):
                return g.tensor_tensor(dst, src, hi, ALU.subtract)

            def unit_part(i, u):
                pool.wait_ge(unit_hi, i * 6 + (u + 1))
                src, hi = unit_view(u), stack_view(u, HI)
                for n in range(2):
                    last = lo_part(stack_view(u, LO)[n], src, hi[n])
                last.then_inc(unit_lo, 1)

            def prob_lo(j, q):
                pool.wait_ge(p_hi, j * 4 + (q + 1))
                at = slice(8 * q, 8 * q + 8)
                for n in range(2):
                    last = lo_part(p_stack[:, at, 2 + n, :], p_c[:, at, :], p_stack[:, at, n, :])
                last.then_inc(p_lo, 1)

            def context_lo(j):
                pool.wait_ge(ctx_hi, j + 1)
                lo_part(ctx_parts[:, LO, :, :], ctx_32[:], ctx_parts[:, HI, :, :]).then_inc(ctx_lo, 1)

            def tile_2(i):
                for s in range(QUARTERS):
                    if s == P_AT:
                        for q in range(4):
                            prob_lo(i - 1, q)
                    if s % 4 == 3 and projects(i):
                        unit_part(i, s // 4)
                context_lo(i - 1)

            def first_units():
                for u in range(6):
                    unit_part(0, u)

            walk(pool, first_units, tile_2)

            pool.sem_inc(down_added, 2)

            def add_down(at, half, ho):
                pool.wait_ge(down_copied, at * 2 + 2)
                pool.wait_ge(down_added, at + 1)
                buffer = (at if isinstance(at, int) else 8 * half + ho) % 2
                g.tensor_tensor(acc[:, half, ho, :], acc[:, half, ho, :], down_tmp[:, buffer, :],
                                ALU.add).then_inc(down_added, 1)

            with pool.Fori(0, NI - 2) as t:
                for d in range(16):
                    add_down(t * 16 + d, d // 8, d % 8)
            for d in range(EARLY):
                add_down(16 * (NI - 2) + d, 0, d)
            for n, (t, d) in enumerate(TAIL_POOL):
                at = TAIL_FROM + n
                if t == OUT:
                    pool.wait_ge(down_copied, at * 2 + 2)
                    pool.wait_ge(res_loaded[d // 4], 16)
                    g.tensor_tensor(x_res[:, d, :], x_res[:, d, :], down_tmp[:, at % 2, :], ALU.add)\
                        .then_inc(down_added, 1)
                else:
                    add_down(at, d // 8, d % 8)

        @block.sync
        def _(sp):
            sp.dma_start(x_tile[:], x_rows[0:P, :]).then_inc(x_loaded, 16)

            def load_w(w):
                if w >= 4:
                    sp.wait_ge(w_turned, w - 3)
                sp.dma_start(w_rows[:, w % 4, :], (Wq, Wk, Wv)[w // KT][(w % KT) * P:(w % KT + 1) * P, :])\
                    .then_inc(w_loaded[w % 4], 16)

            def load_x(i):
                sp.wait_ge(x_turned, i)
                sp.dma_start(x_tile[:], x_rows[bass.ds(i * P, P), :]).then_inc(x_loaded, 16)

            def store_xt(i):
                sp.wait_ge(x_lo, i + 1)
                anchor(sp)
                src = xt_tile[:, :, :].rearrange("p a b -> p (a b)")[:, bass.ds((i % 2) * (2 * KT * P), 2 * KT * P)]
                sp.dma_start(xt_dram.rearrange("t p a k c -> t p (a k c)")[bass.ds(i, 1), :, :]
                             .rearrange("t p c -> (t p) c"), src).then_inc(xt_stored, 16)

            for w in range(8):
                load_w(w)
            for r, b in enumerate((bq, bk, bv)):
                sp.dma_start(bias_qkv[:, r, :], b.rearrange("(a n) -> a n", a=1).broadcast_to((P, H)))\
                    .then_inc(bias_loaded, 16)
            sp.dma_start(bias_o[:], bo.rearrange("(g p) -> p g", p=P),
                         allow_slow_non_contiguous=True).then_inc(bias_loaded, 16)
            for w in range(8, 3 * KT):
                load_w(w)
                if w == 12:
                    store_xt(0)
                    load_x(1)

            def store_context(j):
                sp.wait_ge(ctx_lo, j + 1)
                anchor(sp)
                sp.dma_start(ctx_dram.rearrange("t p a k c -> t p (a k c)")[bass.ds(j, 1), :, :]
                             .rearrange("t p c -> (t p) c"),
                             ctx_parts[:, :, :, :].rearrange("p a k c -> p (a k c)")).then_inc(ctx_stored, 16)

            def load_context(c):
                sp.dma_start(ctx_t[c % 2].rearrange("p t a k c -> p t (a k c)"),
                             ctx_dram[c * CT:(c + 1) * CT].rearrange("t p a k c -> p t (a k c)"))\
                    .then_inc(ctx_loaded[c % 2], 16)

            def load_wo(n):
                if n >= 2:
                    sp.wait_ge(wo_turned, 2 * (n - 1))
                sp.dma_start(wo_rows[:, n % 2, :], Wo[n * P:(n + 1) * P, :]).then_inc(wo_loaded[n % 2], 16)

            def tile_2(i):
                if not isinstance(i, int) or i + 1 < TT:
                    load_x(i + 1)
                    store_xt(i + 1)
                if not projects(i):
                    for n in range(2, KT):
                        load_wo(n)
                    sp.wait_ge(unit_done, 6 * TT)
                    load_context(1)
                if isinstance(i, int) and i == TT - 1:
                    sp.wait_ge(unit_done, 6 * (TT - 1) + 2)
                    load_wo(0)
                    load_wo(1)
                    sp.wait_ge(ctx_stored, 16 * 2 * CT)
                    load_context(0)
                store_context(i - 1)

            walk(sp, lambda: store_xt(1), tile_2)

            sp.wait_ge(ctx_stored, 16 * TT)
            sp.wait_ge(xt_stored, 16 * TT)
            sp.wait_ge(pv_done, 4 * TT)
            for dst, s_in in ((gate_scale, gate_s), (up_scale, up_s)):
                sp.dma_start(dst[:], s_in.rearrange("(t p) g -> p t g", p=P)).then_inc(scales_loaded, 16)
            sp.dma_start(down_scale[:], down_s.rearrange("(h p) t -> p h t", p=P)).then_inc(scales_loaded, 16)
            for c in range(4):
                if c < 2:
                    sp.wait_ge(proj_done, KT * (c + 1))
                    load_context(c + 2)
                sp.dma_start(xt[:, c * CT:(c + 1) * CT, :, :, :].rearrange("p t a k c -> p t (a k c)"),
                             xt_dram[c * CT:(c + 1) * CT].rearrange("t p a k c -> p t (a k c)"))\
                    .then_inc(xt_loaded, 16)

            sp.wait_ge(proj_done, 3 * KT)

            def load_q(mat, t):
                wait_pos(sp, q_conv[mat], t)
                anchor(sp)
                if mat == DOWN:
                    sp.dma_start(q_raw[:, DOWN, :].rearrange("p (h i) -> p h i", i=P),
                                 down_q[:, bass.ds(t * P, P)].rearrange("(h p) i -> p h i", p=P))\
                        .then_inc(q_loaded[mat], 16)
                else:
                    src = gate_q if mat == GATE else up_q
                    sp.dma_start(q_raw[:, mat, :], src[bass.ds(t * P, P), :]).then_inc(q_loaded[mat], 16)

            for mat in (GATE, UP, DOWN):
                load_q(mat, 0)
            with sp.Fori(1, NI) as t:
                for mat in (GATE, UP, DOWN):
                    load_q(mat, t)

            sp.wait_ge(gu_done, NI * 32)
            for c in range(4):
                sp.dma_start(x_res[:, 4 * c:4 * c + 4, :],
                             x_rows[4 * c * P:4 * (c + 1) * P, :].rearrange("(t p) h -> p t h", p=P))\
                    .then_inc(res_loaded[c], 16)
            for u in range(TT):
                if by_pool((OUT, u)):
                    sp.wait_ge(down_added, 2 + TAIL_FROM + TAIL_POOL.index((OUT, u)) + 1)
                else:
                    sp.wait_ge(tail_added, TAIL_FAST.index((OUT, u)) + 1)
                sp.dma_start(out_rows[u * P:(u + 1) * P, :], x_res[:, u, :]).then_inc(y_stored, 16)
            sp.wait_ge(y_stored, 16 * TT)


_INS = ["L0_attn_x", "L0_attn_Wq", "L0_attn_bq", "L0_attn_Wk", "L0_attn_bk", "L0_attn_Wv", "L0_attn_bv",
        "L0_attn_Wo", "L0_attn_bo", "L0_ffn_gate_q", "L0_ffn_gate_s", "L0_ffn_up_q", "L0_ffn_up_s",
        "L0_ffn_down_q", "L0_ffn_down_s"]
_OUTS = [((4, 512, 1024), "float32")]


def kernel(**inputs):
    import numpy as _np
    import concourse.bacc as _bacc
    from concourse import mybir as _mybir
    from concourse.bass_utils import run_bass_kernel_spmd as _run

    nc = _bacc.Bacc("TRN2", target_bir_lowering=False, num_devices=1)
    arrays, args = {}, []
    for name in _INS:
        a = _np.ascontiguousarray(inputs[name])
        arrays[f"in_{name}_dram"] = a
        args.append(nc.dram_tensor(f"in_{name}_dram", a.shape, _mybir.dt.from_np(a.dtype), kind="ExternalInput").ap())
    for i, (shape, dtype) in enumerate(_OUTS):
        dt = _mybir.dt.from_np(_np.dtype(dtype))
        args.append(nc.dram_tensor(f"out_{i}_dram", shape, dt, kind="ExternalOutput").ap())
    build(nc, *args)
    r = _run(nc, [arrays], core_ids=[0])
    got = tuple(r.results[0][f"out_{i}_dram"] for i in range(len(_OUTS)))
    return got[0]
```
